# Optimizing a Trainium2 kernel written in Bass

```python
import numpy as np
import jax
import jax.numpy as jnp

def _softmax(x, axis=-1):
    return jax.nn.softmax(x, axis=axis)

def _gelu(x):
    return jax.nn.gelu(x, approximate=True)

def _silu(x):
    return jax.nn.silu(x)

def _sigmoid(x):
    return jax.nn.sigmoid(x)

def _layernorm(x, axis=-1, eps=1e-05):
    m = jnp.mean(x, axis=axis, keepdims=True)
    v = jnp.var(x, axis=axis, keepdims=True)
    return (x - m) / jnp.sqrt(v + eps)

def _scatter_add(tgt, idx, src, axis=0):
    return tgt.at[idx].add(src)

def _segment_sum(src, seg, n):
    return jax.ops.segment_sum(src, seg, n)
kernel_name = 'mk_seq_preln_d1_jaxref_r8_28afbf'

def setup_inputs(seed: int=0):
    np.random.seed(seed)
    _w = jnp.asarray

    def _L0_attn_setup():
        import jax, jax.numpy as jnp
        import numpy as np
        B, L, C = (2, 256, 128)
        H, POS = (8, 16)
        D = C // H
        MAXS = 32
        S = MAXS + 1
        MAX_FREQ, MIN_FREQ = (16.0, 1.0)
        SCALE = POS ** (-0.5)
        key = jax.random.key(seed)
        ks = jax.random.split(key, 12)

        def w(k, shape, s=0.02):
            return jax.random.normal(k, shape, dtype=jnp.float32) * s
        return {'x': jax.random.normal(ks[0], (B, L, C), dtype=jnp.float32), 'w_wave': w(ks[1], (C, 3 * H)), 'b_wave': w(ks[2], (3 * H,)), 'w_query': w(ks[3], (C, H * POS)), 'b_query': w(ks[4], (H * POS,)), 'key_weight': w(ks[5], (POS,)), 'w_se1': w(ks[6], (C, C // 4)), 'b_se1': w(ks[7], (C // 4,)), 'w_se2': w(ks[8], (C // 4, C)), 'b_se2': w(ks[9], (C,)), 'w_out': w(ks[10], (C, C))}
    _L0_attn_in = _L0_attn_setup()

    def _L0_ffn_setup():
        import jax, jax.numpy as jnp
        import numpy as np
        D_MODEL = 128
        N_EXPERTS = 8
        TOP_K = 2
        HIDDEN = 4 * D_MODEL
        key = jax.random.key(seed)
        ks = jax.random.split(key, 6)
        B, S = (2, 256)
        x = jax.random.normal(ks[0], (B, S, D_MODEL), dtype=jnp.float32)
        shared_w1 = jax.random.normal(ks[1], (HIDDEN, D_MODEL), dtype=jnp.float32) * 0.02
        shared_w2 = jax.random.normal(ks[2], (D_MODEL, HIDDEN), dtype=jnp.float32) * 0.02
        experts_w1 = jax.random.normal(ks[3], (N_EXPERTS, HIDDEN, D_MODEL), dtype=jnp.float32) * 0.02
        experts_w2 = jax.random.normal(ks[4], (N_EXPERTS, D_MODEL, HIDDEN), dtype=jnp.float32) * 0.02
        gate_w = jax.random.normal(ks[5], (N_EXPERTS, D_MODEL), dtype=jnp.float32) * 0.02
        return {'x': x, 'shared_w1': shared_w1, 'shared_w2': shared_w2, 'experts_w1': experts_w1, 'experts_w2': experts_w2, 'gate_w': gate_w}
    _L0_ffn_in = _L0_ffn_setup()
    _d = {'L0_attn_x': _L0_attn_in['x'], 'L0_attn_w_wave': _L0_attn_in['w_wave'], 'L0_attn_b_wave': _L0_attn_in['b_wave'], 'L0_attn_w_query': _L0_attn_in['w_query'], 'L0_attn_b_query': _L0_attn_in['b_query'], 'L0_attn_key_weight': _L0_attn_in['key_weight'], 'L0_attn_w_se1': _L0_attn_in['w_se1'], 'L0_attn_b_se1': _L0_attn_in['b_se1'], 'L0_attn_w_se2': _L0_attn_in['w_se2'], 'L0_attn_b_se2': _L0_attn_in['b_se2'], 'L0_attn_w_out': _L0_attn_in['w_out'], 'L0_ffn_shared_w1': _L0_ffn_in['shared_w1'], 'L0_ffn_shared_w2': _L0_ffn_in['shared_w2'], 'L0_ffn_experts_w1': _L0_ffn_in['experts_w1'], 'L0_ffn_experts_w2': _L0_ffn_in['experts_w2'], 'L0_ffn_gate_w': _L0_ffn_in['gate_w']}
    _x0 = _d['L0_attn_x']
    _d['L0_attn_x'] = jax.random.normal(jax.random.fold_in(jax.random.key(seed), 1), (8, 1024, 128), dtype=_x0.dtype)
    del _x0
    return _d

def reference(L0_attn_x, L0_attn_w_wave, L0_attn_b_wave, L0_attn_w_query, L0_attn_b_query, L0_attn_key_weight, L0_attn_w_se1, L0_attn_b_se1, L0_attn_w_se2, L0_attn_b_se2, L0_attn_w_out, L0_ffn_shared_w1, L0_ffn_shared_w2, L0_ffn_experts_w1, L0_ffn_experts_w2, L0_ffn_gate_w):

    def _L0_attn_ref(x, w_wave, b_wave, w_query, b_query, key_weight, w_se1, b_se1, w_se2, b_se2, w_out):
        import jax, jax.numpy as jnp
        import numpy as np
        B, L, C = (2, 256, 128)
        H, POS = (8, 16)
        D = C // H
        MAXS = 32
        S = MAXS + 1
        MAX_FREQ, MIN_FREQ = (16.0, 1.0)
        SCALE = POS ** (-0.5)
        b, l, c = x.shape
        stride_grid = jnp.arange(-MAXS // 2, MAXS // 2 + 1, dtype=x.dtype)
        wp = jax.nn.silu(x @ w_wave + b_wave).reshape(b, l, 3, H)
        freq = jax.nn.sigmoid(wp[:, :, 0, :]) * (MAX_FREQ - MIN_FREQ) + MIN_FREQ
        phase = jnp.tanh(wp[:, :, 1, :]) * MAX_FREQ
        decay = jax.nn.sigmoid(wp[:, :, 2, :]) * 9.5 + 0.5
        freq_avg = freq.mean(-1)
        phase_avg = phase.mean(-1)
        decay_avg = decay.mean(-1)
        q = jax.nn.silu(x @ w_query + b_query).reshape(b, l, H, POS)
        centers = jnp.arange(l, dtype=x.dtype)
        sample_pos = centers[None, :, None] + stride_grid[None, None, :] * freq_avg[..., None] + phase_avg[..., None]
        valid = (sample_pos >= 0) & (sample_pos < l)
        idx = jnp.clip(sample_pos.astype(jnp.int32), 0, l - 1)
        values = jnp.take_along_axis(x[:, :, None, :], idx[:, :, :, None], axis=1)
        values = values.reshape(b, l, S, H, D).transpose(0, 1, 3, 2, 4)
        rel = jnp.abs(stride_grid)[None, None, None, :] * freq_avg[:, :, None, None]
        qk = jnp.einsum('blhd,d->blh', q, key_weight)
        scores = qk[..., None] * rel * SCALE
        env = jnp.exp(-rel / jnp.clip(decay_avg, 0.1, None)[:, :, None, None])
        mask = valid[:, :, None, :]
        scores = jnp.where(mask, scores, -jnp.inf)
        attn = jax.nn.softmax(scores, axis=-1) * env * mask.astype(x.dtype)
        attn = attn / (attn.sum(-1, keepdims=True) + 1e-08)
        out = jnp.einsum('blhsd,blhs->blhd', values, attn).reshape(b, l, c)
        se = jax.nn.sigmoid(jax.nn.silu(out @ w_se1 + b_se1) @ w_se2 + b_se2)
        out = out * se
        out = jax.nn.silu(out @ w_out)
        return out

    def _L0_ffn_ref(x, shared_w1, shared_w2, experts_w1, experts_w2, gate_w):
        import jax, jax.numpy as jnp
        import numpy as np
        D_MODEL = 128
        N_EXPERTS = 8
        TOP_K = 2
        HIDDEN = 4 * D_MODEL
        B, S, D = x.shape
        T = B * S
        x_flat = x.reshape(T, D)
        shared = jnp.einsum('td,dh->th', x_flat, shared_w1.T)
        shared = jnp.einsum('th,hd->td', jax.nn.silu(shared), shared_w2.T)
        gate_logits = x_flat @ gate_w.T
        top_k_gates, top_k_idx = jax.lax.top_k(gate_logits, TOP_K)
        top_k_gates = jax.nn.softmax(top_k_gates, axis=1)
        gates = jnp.zeros((T, N_EXPERTS), dtype=x.dtype)
        gates = gates.at[jnp.arange(T)[:, None], top_k_idx].set(top_k_gates)
        h = jnp.einsum('td,ehd->teh', x_flat, experts_w1)
        expert_out = jnp.einsum('teh,edh->ted', jax.nn.silu(h), experts_w2)
        selected = jnp.einsum('ted,te->td', expert_out, gates)
        return (shared + selected).reshape(B, S, D)
    x = L0_attn_x
    x = x + _L0_attn_ref(_layernorm(x, axis=-1), L0_attn_w_wave, L0_attn_b_wave, L0_attn_w_query, L0_attn_b_query, L0_attn_key_weight, L0_attn_w_se1, L0_attn_b_se1, L0_attn_w_se2, L0_attn_b_se2, L0_attn_w_out)
    x = x + _L0_ffn_ref(_layernorm(x, axis=-1), L0_ffn_shared_w1, L0_ffn_shared_w2, L0_ffn_experts_w1, L0_ffn_experts_w2, L0_ffn_gate_w)
    return x

_drawn_inputs = setup_inputs


def setup_inputs(seed=0):
    import zlib

    import numpy as np

    out = dict(_drawn_inputs(seed))
    spreads = {}
    factors = {'L0_attn_b_wave': 21.814,
     'L0_attn_w_query': 8.0,
     'L0_attn_b_query': 64.0,
     'L0_attn_key_weight': 22.98,
     'L0_attn_w_se1': 62.793,
     'L0_attn_b_se1': 64.0,
     'L0_attn_w_se2': 58.52,
     'L0_attn_b_se2': 64.0}
    for name, (base, spread) in spreads.items():
        noise = np.random.default_rng([zlib.crc32(name.encode()), seed]).standard_normal(out[name].shape)
        drawn = base * np.exp(spread * noise) if base else spread * noise
        out[name] = jnp.asarray(drawn.astype(out[name].dtype))
    for name, factor in factors.items():
        out[name] = (out[name] * factor).astype(out[name].dtype)
    return out
```

```python
from contextlib import ExitStack

import concourse.bass as bass
from concourse import mybir


def build_program(nc, x, w_wave, b_wave, w_query, b_query, key_weight, w_se1, b_se1, w_se2, b_se2,
                  w_out, shared_w1, shared_w2, experts_w1, experts_w2, gate_w, out):
    F32, F32R, BF16 = mybir.dt.float32, mybir.dt.float32r, mybir.dt.bfloat16
    U32 = mybir.dt.uint32
    ALU = mybir.AluOpType
    ACT = mybir.ActivationFunctionType
    AX = mybir.AxisListType.X

    P = 128
    B, L, C = x.shape
    NT = L // P
    NH = w_wave.shape[1] // 3
    D = C // NH
    NW, NQ = w_wave.shape[1], w_query.shape[1]
    NP = NW + NQ
    MAXK = 16
    NK = MAXK + 1
    NE = experts_w1.shape[0]
    HID = experts_w1.shape[1]
    NHC = HID // P
    HALF = L // 2
    EPS = 1e-5
    LOW_ROWS, HIGH_ROWS = 8, 16
    LOW = 2 * P + LOW_ROWS
    HIGH = 3 * P + HIGH_ROWS
    WMAX = LOW + HIGH
    MAGIC = float(3 * 2 ** 22)
    NU = 2 * (NE + 1)

    def window(lb):
        lo = max(0, lb * P - LOW) if lb >= 3 else 0
        return lo, min(L, lb * P + HIGH) - lo

    def pieces(lb):
        return list(range(max(0, lb - 2), min(NT, lb + 3)))

    def slots(lb):
        full = [("chunk", c) for c in pieces(lb)]
        tails = [("tails", 0)] if (lb >= 3 or lb + 3 < NT) else []
        return full[:1] + tails + full[1:]

    SLOTS_BEFORE = [2 * sum(len(slots(k)) for k in range(lb)) for lb in range(NT + 1)]

    ctx = ExitStack()
    with ctx:
        def sb(name, shape, dt=F32):
            return ctx.enter_context(nc.sbuf_tensor(name, shape, dt))

        def sem(name):
            return ctx.enter_context(nc.semaphore(name))

        ident = sb("ident", [P, P])
        ident_bf = sb("ident_bf", [P, P], BF16)
        rows = sb("rows", [P, L])
        centers = sb("centers", [P, NT])
        strides = sb("strides", [P, 2 * MAXK + 1])
        falling = sb("falling", [P, NK])
        minus_half = sb("minus_half", [P, NT])
        expert_ids = sb("expert_ids", [P, NE])
        w_proj = sb("w_proj", [P, NP])
        bias_proj = sb("bias_proj", [P, NP])
        key_w = sb("key_w", [P, NH, D])
        se1_w = sb("se1_w", [P, C // 4])
        se2_w = sb("se2_w", [C // 4, C])
        se1_b = sb("se1_b", [C // 4, 2])
        se2_b = sb("se2_b", [C, 2])
        out_w = sb("out_w", [P, C])
        gate_raw = sb("gate_raw", [NE, C])
        gate_wT = sb("gate_wT", [P, NE])
        w1_hi = sb("w1_hi", [P, NE + 1, HID], F32R)
        w1_lo = sb("w1_lo", [P, NE + 1, HID], F32R)
        w2T = sb("w2T", [P, NE + 1, NHC, C])

        x_in = sb("x_in", [P, NT, C])
        x_res = sb("x_res", [P, NT, C])
        xn = sb("xn", [P, NT, C])
        xn_last = sb("xn_last", [LOW_ROWS, NT, C])
        xnT = sb("xnT", [P, L])
        proj = sb("proj", [P, NT, NP])
        stats = sb("stats", [P, NT, 6])
        mean_var = sb("mean_var", [P, NT, 2])
        var_eps = sb("var_eps", [P, NT])
        rstd = sb("rstd", [P, NT])
        wave = sb("wave", [P, NT, 3, NH])
        wave_sum = sb("wave_sum", [P, NT, 3])
        freq = sb("freq", [P, NT])
        phase = sb("phase", [P, NT])
        decay = sb("decay", [P, NT])
        rfreq = sb("rfreq", [P, NT])
        rdecay = sb("rdecay", [P, NT])
        freq_decay = sb("freq_decay", [P, NT])
        shift = sb("shift", [P, NT])
        shift2 = sb("shift2", [P, NT])
        qk = sb("qk", [P, NT, NH])
        slopes = sb("slopes", [P, 2, NT, NH])
        end1 = sb("end1", [P, NT, NH])
        end2 = sb("end2", [P, NT, NH])
        neg_max = sb("neg_max", [P, NT, NH])
        pos = sb("pos", [P, NT, 2 * MAXK + 1])
        valid = sb("valid", [P, NT, 2 * MAXK + 1])
        some = sb("some", [P, NT, NK])
        some2 = sb("some2", [P, NT, NK])
        kmax = sb("kmax", [P, NT])
        kmin = sb("kmin", [P, NT])
        sums = sb("sums", [P, 2, NT * NH, NK])
        half_tanh = sums[:].rearrange("p a n k -> p (a n k)")[:, 0:NT * NP].rearrange("p (t n) -> p t n", t=NT)
        sum_zu = sb("sum_zu", [P, 2, NT * NH])
        denom = sb("denom", [P, NT * NH])
        rdenom = sb("rdenom", [P, NT * NH])

        samp = sb("samp", [P, 2, WMAX])
        place = sb("place", [P, 2, WMAX])
        dist = sb("dist", [P, 2, WMAX])
        not_below = sb("not_below", [P, WMAX], BF16)
        hit = sb("hit", [P, 2, WMAX], BF16)
        hitT = sb("hitT", [P, 2, 7, P], BF16)
        weight = sb("weight", [P, 2, NH, WMAX])
        weightT = sb("weightT", [P, 3, 4, P])
        mixT = sb("mixT", [P, 2, P])
        mix = x_in[:].rearrange("p t (h d) -> p t h d", d=D)

        x1 = sb("x1", [P, NT, C])
        acc = sb("acc", [P, NT, C])
        xT_hi = sb("xT_hi", [P, L], F32R)
        xT_lo = sb("xT_lo", [P, L], F32R)
        hidden = sb("hidden", [P, 2, NHC, HALF])
        gates = sb("gates", [P, NT, NE])
        logits = sb("logits", [P, NT, NE])
        top = sb("top", [P, NT, 8])
        top_id = sb("top_id", [P, NT, 8], U32)
        top_idf = sb("top_idf", [P, NT, 8])
        gate12 = sb("gate12", [P, 2, NT])
        picked = logits

        raw_w1 = weight[:, 0, :, :].rearrange("p h w -> p (h w)")[:, 0:(NE + 1) * HID].rearrange(
            "p (e k d) -> p e k d", e=NE + 1, d=C)
        raw_w2 = weight[:, 1, :, :].rearrange("p h w -> p (h w)")[:, 0:(NE + 1) * HID].rearrange(
            "p (e h) -> p e h", e=NE + 1)
        late = weight[:, 0, :, :].rearrange("p h w -> p (h w)")
        se_tanh, se_lin = late[0:C // 4, 0:L], late[0:C // 4, L:2 * L]
        se_gate, out_tanh, attn = late[:, 2 * L:3 * L], late[:, 3 * L:4 * L], late[:, 4 * L:5 * L]
        late2 = weight[:, 1, :, :].rearrange("p h w -> p (h w)")
        xn2 = late2[:, 0:L].rearrange("p (t c) -> p t c", t=NT)
        xn2T = late2[:, L:2 * L]

        bank = [ctx.enter_context(nc.psum_tensor(f"bank{i}", [P, 512], F32)) for i in range(8)]
        turn = bank[0:2]
        mixed = bank[2]
        misc = bank[3]
        up = bank[4:6]

        def tail_hits(which):
            n = (LOW_ROWS, HIGH_ROWS)[which]
            return misc[0:n, 5 * P // 2 + 32 * which:5 * P // 2 + 32 * (which + 1)]

        down = bank[6:8]

        names = ("setup_consts setup_act setup_dve raw_loaded small_loaded gate_turned "
                 "weights_turned weights_hi weights_free "
                 "x_loaded res_loaded var_ready rstd_ready xn_ready last_copied xn_turned xnT_ready "
                 "proj_done proj_ready tanh_ready silu_ready wave_ready geometry params sums_ready "
                 "sums_exp sums_masked candidates dist_ready hit_ready hit_turned hitT_ready "
                 "weight_ready turned maskedT mixed_slot mixT_ready mix_turned mix_ready "
                 "mix_scaled mix2_turned mix2T_ready se1_done se1_tanh se1_ready se2_done se2_tanh "
                 "gated out_done out_tanh_ready x1_ready xn2_ready xn2_turned xn2T_ready hi_ready lo_ready "
                 "logits_done gap_ready gap_exp up_done silu_done down_done acc_done stored "
                 "dve_seq pool_seq").split()
        s = {n: sem(n) for n in names}

        x_dram = x.rearrange("b (t p) c -> p (b t) c", p=P)
        out_dram = out.rearrange("b (t p) c -> p (b t) c", p=P)

        class Chain:

            def __init__(self, eng, sem):
                self.eng, self.sem, self.n = eng, sem, 0

            def __call__(self, ins):
                self.n += 1
                ins.then_inc(self.sem, 1)

            def wait(self):
                self.eng.wait_ge(self.sem, self.n)

        def clear_semaphores():
            with nc.Block(no_gpsimd_drain=True) as block:
                @block.sync
                def _(sp):
                    for n in names:
                        sp.sem_clear(s[n])

        def setup():
            with nc.Block() as block:
                @block.sync
                def _(sp):
                    for e in range(NE):
                        sp.dma_start(raw_w1[:, e], experts_w1[e].rearrange("(k p) d -> p k d", p=P)
                                     ).then_inc(s["raw_loaded"], 16)
                    sp.dma_start(raw_w1[:, NE], shared_w1.rearrange("(k p) d -> p k d", p=P)
                                 ).then_inc(s["raw_loaded"], 16)
                    sp.dma_start(raw_w2[:, 0:NE], experts_w2.rearrange("e d h -> d e h")
                                 ).then_inc(s["raw_loaded"], 16)
                    sp.dma_start(raw_w2[:, NE], shared_w2).then_inc(s["raw_loaded"], 16)

                @block.gpsimd
                def _(pool):
                    seq = Chain(pool, s["pool_seq"])
                    nc.gpsimd.memset(ident[:], 0.0)
                    seq(nc.gpsimd.memset(ident_bf[:], 0.0))
                    seq.wait()
                    for m in (ident, ident_bf):
                        nc.gpsimd.affine_select(out=m[:], in_=m[:], compare_op=ALU.not_equal, fill=1.0,
                                                base=0, pattern=[[-1, P]], channel_multiplier=1)
                    nc.gpsimd.memset(minus_half[:], -0.5)
                    iota = dict(allow_small_or_imprecise_dtypes=True)
                    nc.gpsimd.iota(rows[:], [[1, L]], base=0, channel_multiplier=0, **iota)
                    nc.gpsimd.iota(centers[:], [[P, NT]], base=0, channel_multiplier=1, **iota)
                    nc.gpsimd.iota(strides[:, 0:NK], [[1, NK]], base=0, channel_multiplier=0, **iota)
                    nc.gpsimd.iota(strides[:, NK:], [[-1, MAXK]], base=-1, channel_multiplier=0, **iota)
                    nc.gpsimd.iota(falling[:], [[-1, NK]], base=MAXK, channel_multiplier=0, **iota)
                    nc.gpsimd.iota(expert_ids[:], [[1, NE]], base=0, channel_multiplier=0,
                                   **iota).then_inc(s["setup_consts"], 1)

                @block.scalar
                def _(act):
                    small = [(w_proj[:, 0:NW], w_wave), (w_proj[:, NW:NP], w_query),
                             (bias_proj[:, 0:NW], b_wave.partition_broadcast(P)),
                             (bias_proj[:, NW:NP], b_query.partition_broadcast(P)),
                             (key_w[:, 0, :], key_weight.partition_broadcast(P)),
                             (se1_w[:], w_se1), (se2_w[:], w_se2),
                             (se1_b[:, 0:1], b_se1.rearrange("(p a) -> p a", a=1)),
                             (se2_b[:, 0:1], b_se2.rearrange("(p a) -> p a", a=1)),
                             (out_w[:], w_out), (gate_raw[:], gate_w)]
                    for dst, src in small:
                        act.dma_start(dst, src).then_inc(s["small_loaded"], 16)
                    for g in range(2 * (NE + 1)):
                        act.wait_ge(s["weights_turned"], g + 1)
                        e = g % (NE + 1)
                        dst = w1_hi[:, e, :] if g <= NE else w2T[:, e].rearrange("p k d -> p (k d)")
                        nc.scalar.activation(dst, turn[g % 2][:], ACT.Copy).then_inc(s["weights_hi"], 1)
                    act.wait_ge(s["gate_turned"], 1)
                    nc.scalar.activation(gate_wT[:], misc[:, 0:NE], ACT.Copy)

                @block.tensor
                def _(pe):
                    pe.wait_ge(s["setup_consts"], 1)
                    pe.wait_ge(s["raw_loaded"], 16 * (NE + 3))
                    for g in range(2 * (NE + 1)):
                        e = g % (NE + 1)
                        if g >= 2:
                            pe.wait_ge(s["weights_hi"], g - 1)
                            pe.wait_ge(s["weights_free"], min(g - 1, NE + 1))
                        for k in range(NHC):
                            src = raw_w1[:, e, k, :] if g <= NE else raw_w2[:, e, k * P:(k + 1) * P]
                            ins = nc.tensor.transpose(turn[g % 2][:, k * P:(k + 1) * P], src, ident[:])
                        ins.then_inc(s["weights_turned"], 1)
                    pe.wait_ge(s["small_loaded"], 16 * 11)
                    nc.tensor.transpose(misc[:, 0:NE], gate_raw[:], ident[0:NE, 0:NE]
                                        ).then_inc(s["gate_turned"], 1)

                @block.vector
                def _(dve):
                    for g in range(NE + 1):
                        dve.wait_ge(s["weights_hi"], g + 1)
                        nc.vector.tensor_tensor(w1_lo[:, g, :], turn[g % 2][:],
                                                w1_hi[:, g, :].bitcast(F32), ALU.subtract
                                                ).then_inc(s["weights_free"], 1)
                    dve.wait_ge(s["small_loaded"], 16 * 11)
                    for h in range(1, NH):
                        nc.vector.tensor_copy(key_w[:, h, :], key_w[:, 0, :])
                    nc.vector.tensor_scalar(se1_b[:, 1:2], se1_b[:, 0:1], 0.5, None, ALU.mult)
                    nc.vector.tensor_scalar(se2_b[:, 1:2], se2_b[:, 0:1], 0.5, None, ALU.mult)
                    nc.vector.tensor_scalar(out_w[:], out_w[:], 0.5, None, ALU.mult)

        def step(b, attention, ffn):
            plan = []
            units = [("ffn", m) for m in range(NU + 1)] if ffn else []
            if attention:
                marks = ([("prep", 0), ("base", 0), ("exp", 0), ("base", 1), ("sums", 0)]
                         + [t for lb in range(NT) for t in
                            ([("exp", lb + 1)] * (lb + 1 < NT) + [("base", lb + 2)] * (lb + 2 < NT)
                             + [("mix", lb)])])
                first = 3
                plan += units[:first]
                units = units[first:]
                plan += marks[:5]
                per = [2, 2, 2, 2, 2, 2, 2, 2]
                for t in marks[5:]:
                    plan.append(t)
                    if t[0] == "mix":
                        n = per[t[1]] if t[1] < NT - 1 else len(units)
                        plan += units[:n]
                        units = units[n:]
                plan.append(("post", 0))
            else:
                plan += units

            def expert_of(m):
                return m // (NE + 1), (m - 1) % (NE + 1) if m % (NE + 1) else NE

            with nc.Block(no_gpsimd_drain=True) as block:

                @block.sync
                def _(sp):
                    if attention:
                        for q in range(4):
                            sp.dma_start(x_in[:, 2 * q:2 * q + 2], x_dram[:, bass.ds(b * NT + 2 * q, 2), :]
                                         ).then_inc(s["x_loaded"], 16)
                        sp.dma_start(x_res[:], x_dram[:, bass.ds(b * NT, NT), :]).then_inc(s["res_loaded"], 16)
                        sp.wait_ge(s["xn_ready"], 1)
                        sp.dma_start(xn_last[:], xn[P - LOW_ROWS:P]).then_inc(s["last_copied"], 16)
                        sp.wait_ge(s["last_copied"], 16)
                        sp.wait_ge(s["res_loaded"], 16)
                    if ffn:
                        for hf in range(2):
                            sp.wait_ge(s["acc_done"], (NE + 1) * (hf + 1))
                            sp.dma_start(out_dram[:, bass.ds((b - 1) * NT + hf * NT // 2, NT // 2), :],
                                         acc[:, hf * NT // 2:(hf + 1) * NT // 2]).then_inc(s["stored"], 16)
                        sp.wait_ge(s["stored"], 32)

                @block.gpsimd
                def _(pool):
                    seq = Chain(pool, s["pool_seq"])

                    def reciprocal_root(n):
                        pool.wait_ge(s["var_ready"], n)
                        nc.gpsimd.tensor_tensor(rstd[:], var_eps[:], minus_half[:], ALU.pow
                                                ).then_inc(s["rstd_ready"], 1)

                    def base(lb):
                        lo, w = window(lb)
                        k = lb % 2
                        pool.wait_ge(s["geometry"], 1)
                        if lb >= 2:
                            pool.wait_ge(s["dist_ready"], lb - 1)
                            pool.wait_ge(s["hit_ready"], lb - 1)
                        r = samp[:, k, 0:w]
                        seq(nc.gpsimd.tensor_scalar(r, rows[:, lo:lo + w], rfreq[:, lb:lb + 1],
                                                    shift2[:, lb:lb + 1], ALU.mult, ALU.add))
                        seq.wait()
                        seq(nc.gpsimd.tensor_scalar(r, r, float(MAXK), float(-MAXK), ALU.min, ALU.max))
                        seq.wait()
                        seq(nc.gpsimd.tensor_scalar(r, r, MAGIC, 1.0, ALU.add, ALU.mult))
                        seq.wait()
                        seq(nc.gpsimd.tensor_scalar(r, r, 1.0, -MAGIC, ALU.mult, ALU.add))
                        seq.wait()
                        nc.gpsimd.tensor_scalar(place[:, k, 0:w], r, freq[:, lb:lb + 1],
                                                centers[:, lb:lb + 1], ALU.mult, ALU.add
                                                ).then_inc(s["candidates"], 1)

                    def terms():
                        pool.wait_ge(s["params"], 1)
                        flat = sums[:].rearrange("p a n k -> p (a n) k")
                        n2 = 2 * NT * NH
                        seq(nc.gpsimd.tensor_tensor(
                            flat, slopes[:].rearrange("p a t h -> p (a t h)").unsqueeze(2).broadcast_to([P, n2, NK]),
                            strides[:, 0:NK].unsqueeze(1).broadcast_to([P, n2, NK]), ALU.mult))
                        seq.wait()
                        for a in range(2):
                            seq(nc.gpsimd.tensor_tensor(
                                sums[:, a], sums[:, a],
                                neg_max[:].rearrange("p t h -> p (t h)").unsqueeze(2).broadcast_to([P, NT * NH, NK]),
                                ALU.add))
                        seq.wait()
                        nc.gpsimd.tensor_scalar(flat, flat, 0.0, 0.0, ALU.min, ALU.add
                                                ).then_inc(s["sums_ready"], 1)
                        pool.wait_ge(s["sums_exp"], 1)
                        for a in range(2):
                            v = sums[:, a].rearrange("p (t h) k -> p t h k", t=NT)
                            ins = nc.gpsimd.tensor_tensor(
                                v, v, some[:].unsqueeze(2).broadcast_to([P, NT, NH, NK]), ALU.mult)
                        ins.then_inc(s["sums_masked"], 1)

                    for what, n in plan:
                        if what == "prep":
                            reciprocal_root(1)
                        elif what == "base":
                            base(n)
                        elif what == "sums":
                            terms()
                        elif what == "post":
                            reciprocal_root(2)

                @block.scalar
                def _(act):
                    def copy(dst, src):
                        return nc.scalar.activation(dst, src, ACT.Copy)

                    def prep():
                        for i in range(2):
                            act.wait_ge(s["xn_turned"], i + 1)
                            copy(xnT[:, i * HALF:(i + 1) * HALF], turn[i][:]).then_inc(s["xnT_ready"], 1)
                        act.wait_ge(s["proj_ready"], 3)
                        nc.scalar.activation(half_tanh, proj[:], ACT.Tanh, scale=0.5
                                             ).then_inc(s["tanh_ready"], 1)
                        act.wait_ge(s["silu_ready"], 1)
                        wv = proj[:, :, 0:NW].rearrange("p t (k h) -> p t k h", k=3)
                        nc.scalar.activation(wave[:, :, 0:3:2, :], wv[:, :, 0:3:2, :], ACT.Tanh, scale=0.5)
                        nc.scalar.activation(wave[:, :, 1, :], wv[:, :, 1, :], ACT.Tanh
                                             ).then_inc(s["wave_ready"], 1)

                    def exps(lb):
                        w = window(lb)[1]
                        act.wait_ge(s["params"], 1)
                        act.wait_ge(s["dist_ready"], lb + 1)
                        if lb >= 2:
                            act.wait_ge(s["turned"], SLOTS_BEFORE[lb - 1])
                        for h in range(NH):
                            nc.scalar.activation(weight[:, lb % 2, h, 0:w], dist[:, lb % 2, 0:w], ACT.Exp,
                                                 scale=slopes[:, 1, lb, h:h + 1], bias=neg_max[:, lb, h:h + 1]
                                                 ).then_inc(s["weight_ready"], 1)

                    def sums_exp():
                        act.wait_ge(s["sums_ready"], 1)
                        flat = sums[:].rearrange("p a n k -> p (a n k)")
                        nc.scalar.activation(flat, flat, ACT.Exp).then_inc(s["sums_exp"], 1)

                    def mix_copy(lb):
                        act.wait_ge(s["mixed_slot"], SLOTS_BEFORE[lb + 1])
                        if lb:
                            act.wait_ge(s["mix_turned"], lb)
                        copy(mixT[:].rearrange("p a l -> p (a l)"), mixed[:, 0:2 * P]).then_inc(s["mixT_ready"], 1)

                    def unit(m):
                        if m == NU:
                            return
                        if m >= 2:
                            act.wait_ge(s["down_done"], m - 1)
                        for k in range(NHC):
                            n = m * NHC + k
                            act.wait_ge(s["up_done"], n + 1)
                            nc.scalar.activation(hidden[:, m % 2, k, :], up[n % 2][:], ACT.Silu
                                                 ).then_inc(s["silu_done"], 1)

                    def post():
                        for i in range(2):
                            act.wait_ge(s["mix2_turned"], i + 1)
                            copy(xnT[:, i * HALF:(i + 1) * HALF], turn[i][:]).then_inc(s["mix2T_ready"], 1)
                        for i, ps in enumerate((misc, mixed)):
                            act.wait_ge(s["se1_done"], i + 1)
                            nc.scalar.activation(se_tanh[:, i * HALF:(i + 1) * HALF], ps[0:C // 4, :], ACT.Tanh,
                                                 scale=0.5, bias=se1_b[:, 1:2]).then_inc(s["se1_tanh"], 1)
                        for i in range(2):
                            act.wait_ge(s["se2_done"], i + 1)
                            nc.scalar.activation(se_gate[:, i * HALF:(i + 1) * HALF], turn[i][:], ACT.Tanh,
                                                 scale=0.5, bias=se2_b[:, 1:2]).then_inc(s["se2_tanh"], 1)
                        for i in range(2):
                            act.wait_ge(s["out_done"], i + 1)
                            nc.scalar.activation(out_tanh[:, i * HALF:(i + 1) * HALF], turn[i][:], ACT.Tanh,
                                                 scale=0.5).then_inc(s["out_tanh_ready"], 1)
                        if ffn:
                            act.wait_ge(s["up_done"], NU * NHC)
                        for i in range(2):
                            act.wait_ge(s["xn2_turned"], i + 1)
                            copy(xT_hi[:, i * HALF:(i + 1) * HALF], turn[i][:]).then_inc(s["hi_ready"], 1)
                            copy(xn2T[:, i * HALF:(i + 1) * HALF], turn[i][:]).then_inc(s["xn2T_ready"], 1)

                        act.wait_ge(s["gap_ready"], 1)
                        nc.scalar.activation(gate12[:, 1], gate12[:, 1], ACT.Exp).then_inc(s["gap_exp"], 1)

                    for what, n in plan:
                        if what == "prep":
                            prep()
                        elif what == "exp":
                            exps(n)
                        elif what == "sums":
                            sums_exp()
                        elif what == "mix":
                            mix_copy(n)
                        elif what == "ffn":
                            unit(n)
                        elif what == "post":
                            post()

                @block.tensor
                def _(pe):
                    def turn_all(src, signal):
                        for t in range(NT):
                            ins = nc.tensor.transpose(turn[t // 4][:, (t % 4) * P:(t % 4 + 1) * P],
                                                      src(t), ident[:])
                            if t % 4 == 3:
                                ins.then_inc(s[signal], 1)

                    def prep():
                        pe.wait_ge(s["xn_ready"], 1)
                        turn_all(lambda t: xn[:, t, :], "xn_turned")
                        pe.wait_ge(s["xnT_ready"], 2)
                        for g, ps in enumerate((turn[0], turn[1], misc)):
                            for t in range(3 * g, min(3 * g + 3, NT)):
                                ins = nc.tensor.matmul(ps[:, (t - 3 * g) * NP:(t - 3 * g + 1) * NP],
                                                       xnT[:, t * P:(t + 1) * P], w_proj[:], start=True, stop=True)
                            ins.then_inc(s["proj_done"], 1)

                    def turn_hits(lb):
                        lo, _ = window(lb)
                        pe.wait_ge(s["hit_ready"], lb + 1)
                        if lb:
                            pe.wait_ge(s["mix_ready"], lb)
                        else:
                            pe.wait_ge(s["proj_ready"], 3)
                        ps = misc[:].bitcast(BF16)
                        h = hit[:, lb % 2, :]
                        for i, c in enumerate(pieces(lb)):
                            ins = nc.tensor.transpose(ps[:, i * P:(i + 1) * P], h[:, c * P - lo:(c + 1) * P - lo],
                                                      ident_bf[:])
                        if lb >= 3:
                            ins = nc.tensor.matmul(tail_hits(0), h[:, 0:LOW_ROWS], ident_bf[:, 0:32],
                                                   start=True, stop=True)
                        if lb + 3 < NT:
                            at = (lb + 3) * P - lo
                            ins = nc.tensor.matmul(tail_hits(1), h[:, at:at + HIGH_ROWS], ident_bf[:, 96:P],
                                                   start=True, stop=True)
                        ins.then_inc(s["hit_turned"], 1)

                    def mix_block(lb):
                        turn_hits(lb)
                        lo, _ = window(lb)
                        todo = [(hg, i, sl) for hg in range(2) for i, sl in enumerate(slots(lb))]

                        def turn_slot(j):
                            n = SLOTS_BEFORE[lb] + j
                            hg, _, (kind, c) = todo[j]
                            if n >= 2:
                                pe.wait_ge(s["maskedT"], n - 1)
                            pe.wait_ge(s["weight_ready"], NH * lb + 4 * hg + 4)
                            ps = turn[n % 2]
                            for g in range(4):
                                wt = weight[:, lb % 2, 4 * hg + g, :]
                                if kind == "chunk":
                                    ins = nc.tensor.transpose(ps[:, g * P:(g + 1) * P],
                                                              wt[:, c * P - lo:(c + 1) * P - lo], ident[:])
                                else:
                                    if lb >= 3:
                                        ins = nc.tensor.matmul(ps[0:LOW_ROWS, g * 32:(g + 1) * 32],
                                                               wt[:, 0:LOW_ROWS], ident[:, 0:32],
                                                               start=True, stop=True)
                                    if lb + 3 < NT:
                                        at = (lb + 3) * P - lo
                                        ins = nc.tensor.matmul(ps[0:HIGH_ROWS, P + g * 32:P + (g + 1) * 32],
                                                               wt[:, at:at + HIGH_ROWS], ident[:, 96:P],
                                                               start=True, stop=True)
                            ins.then_inc(s["turned"], 1)

                        def mix_slot(j):
                            n = SLOTS_BEFORE[lb] + j
                            hg, i, (kind, c) = todo[j]
                            pe.wait_ge(s["maskedT"], n + 1)
                            if j == 0 and lb:
                                pe.wait_ge(s["mixT_ready"], lb)
                            last = i == len(slots(lb)) - 1
                            for g in range(4):
                                h = 4 * hg + g
                                ch = 32 * (h // 2)
                                q = mixed[32 * g:32 * g + 32, hg * P:(hg + 1) * P]
                                wt = weightT[:, n % 3, :, :].rearrange("p g l -> p (g l)")
                                if kind == "chunk":
                                    ins = nc.tensor.matmul(q, xn[:, c, ch:ch + 32], wt[:, g * P:(g + 1) * P],
                                                           start=i == 0, stop=last)
                                else:
                                    if lb >= 3:
                                        ins = nc.tensor.matmul(q[:, 0:32], xn_last[:, lb - 3, ch:ch + 32],
                                                               wt[0:LOW_ROWS, g * 32:(g + 1) * 32],
                                                               start=False, stop=False)
                                    if lb + 3 < NT:
                                        ins = nc.tensor.matmul(q[:, 96:P], xn[0:HIGH_ROWS, lb + 3, ch:ch + 32],
                                                               wt[0:HIGH_ROWS, P + g * 32:P + (g + 1) * 32],
                                                               start=False, stop=False)
                            ins.then_inc(s["mixed_slot"], 1)

                        pe.wait_ge(s["last_copied"], 16)
                        for j in range(len(todo) + 1):
                            if j < len(todo):
                                turn_slot(j)
                            if j:
                                mix_slot(j - 1)
                        pe.wait_ge(s["mixT_ready"], lb + 1)
                        for hg in range(2):
                            ins = nc.tensor.transpose(misc[:, hg * P:(hg + 1) * P], mixT[:, hg, :], ident[:])
                        ins.then_inc(s["mix_turned"], 1)

                    def unit_up(m):
                        hf, e = expert_of(m)
                        cols = slice(hf * HALF, (hf + 1) * HALF)
                        for k in range(NHC):
                            n = m * NHC + k
                            if n >= 2:
                                pe.wait_ge(s["silu_done"], n - 1)
                            hs = slice(k * P, (k + 1) * P)
                            nc.tensor.matmul(up[n % 2][:], w1_hi[:, e, hs], xT_hi[:, cols], start=True, stop=False)
                            nc.tensor.matmul(up[n % 2][:], w1_hi[:, e, hs], xT_lo[:, cols], start=False, stop=False)
                            nc.tensor.matmul(up[n % 2][:], w1_lo[:, e, hs], xT_hi[:, cols], start=False, stop=True
                                             ).then_inc(s["up_done"], 1)

                    def unit_down(m):
                        _, e = expert_of(m)
                        pe.wait_ge(s["silu_done"], NHC * (m + 1))
                        if m >= 2:
                            pe.wait_ge(s["acc_done"], m - 1)
                        for t in range(NT // 2):
                            for k in range(NHC):
                                ins = nc.tensor.matmul(down[m % 2][:, t * C:(t + 1) * C],
                                                       hidden[:, m % 2, k, t * P:(t + 1) * P], w2T[:, e, k, :],
                                                       start=k == 0, stop=k == NHC - 1)
                        ins.then_inc(s["down_done"], 1)

                    def post():
                        pe.wait_ge(s["mix_scaled"], 1)
                        turn_all(lambda t: mix[:, t, :, :].rearrange("p h d -> p (h d)"), "mix2_turned")
                        for i, ps in enumerate((misc, mixed)):
                            pe.wait_ge(s["mix2T_ready"], i + 1)
                            nc.tensor.matmul(ps[0:C // 4, :], se1_w[:], xnT[:, i * HALF:(i + 1) * HALF],
                                             start=True, stop=True).then_inc(s["se1_done"], 1)
                        for i in range(2):
                            pe.wait_ge(s["se1_ready"], i + 1)
                            nc.tensor.matmul(turn[i][:], se2_w[:], se_lin[:, i * HALF:(i + 1) * HALF],
                                             start=True, stop=True).then_inc(s["se2_done"], 1)
                        for i in range(2):
                            pe.wait_ge(s["gated"], i + 1)
                            for t in range(4):
                                col = i * HALF + t * P
                                ins = nc.tensor.matmul(turn[i][:, t * C:(t + 1) * C], xnT[:, col:col + P],
                                                       out_w[:], start=True, stop=True)
                            ins.then_inc(s["out_done"], 1)
                        pe.wait_ge(s["xn2_ready"], 1)
                        turn_all(lambda t: xn2[:, t, :], "xn2_turned")
                        pe.wait_ge(s["xn2T_ready"], 2)
                        for t in range(NT):
                            ins = nc.tensor.matmul(misc[:, t * NE:(t + 1) * NE], xn2T[:, t * P:(t + 1) * P],
                                                   gate_wT[:], start=True, stop=True)
                        ins.then_inc(s["logits_done"], 1)

                    for what, n in plan:
                        if what == "prep":
                            prep()
                        elif what == "mix":
                            mix_block(n)
                        elif what == "ffn":
                            if n < NU:
                                unit_up(n)
                            if n:
                                unit_down(n - 1)
                        elif what == "post":
                            post()

                @block.vector
                def _(dve):
                    seq = Chain(dve, s["dve_seq"])
                    V = nc.vector

                    def step_of(ins):
                        seq(ins)
                        seq.wait()

                    def over(a, n):
                        return a.unsqueeze(2).broadcast_to([P, a.shape[1], n])

                    def layernorm(src, dst, n, done):
                        for t in range(NT):
                            ins = V.bn_stats(stats[:, t, :], src[:, t, :])
                        step_of(ins)
                        for t in range(NT):
                            ins = V.bn_aggr(mean_var[:, t, :], stats[:, t, :])
                        step_of(ins)
                        V.tensor_scalar(var_eps[:], mean_var[:, :, 1], EPS, None, ALU.add
                                        ).then_inc(s["var_ready"], 1)
                        dve.wait_ge(s["rstd_ready"], n)
                        for t in range(NT):
                            ins = V.tensor_scalar(dst[:, t, :], src[:, t, :], mean_var[:, t, 0:1],
                                                  rstd[:, t:t + 1], ALU.subtract, ALU.mult)
                        ins.then_inc(s[done], 1)

                    def prep():
                        dve.wait_ge(s["x_loaded"], 64)
                        layernorm(x_in, xn, 1, "xn_ready")
                        for g in range(3):
                            nt = min(3, NT - 3 * g)
                            ps = (turn[0], turn[1], misc)[g]
                            dve.wait_ge(s["proj_done"], g + 1)
                            V.tensor_tensor(proj[:, 3 * g:3 * g + nt, :],
                                            ps[:, 0:nt * NP].rearrange("p (t n) -> p t n", n=NP),
                                            bias_proj[:].unsqueeze(1).broadcast_to([P, nt, NP]), ALU.add
                                            ).then_inc(s["proj_ready"], 1)
                        dve.wait_ge(s["tanh_ready"], 1)
                        step_of(V.tensor_scalar(half_tanh, half_tanh, 0.5, 0.5, ALU.mult, ALU.add))
                        V.tensor_tensor(proj[:], proj[:], half_tanh, ALU.mult).then_inc(s["silu_ready"], 1)
                        dve.wait_ge(s["silu_ready"], 1)
                        qw = half_tanh[:, :, 0:NQ]
                        step_of(V.tensor_tensor(qw, proj[:, :, NW:NP],
                                                key_w[:].rearrange("p h d -> p (h d)").unsqueeze(1).broadcast_to([P, NT, NQ]),
                                                ALU.mult))
                        V.tensor_reduce(qk[:], qw.rearrange("p t (h d) -> p t h d", d=D), AX, ALU.add)
                        dve.wait_ge(s["wave_ready"], 1)
                        step_of(V.tensor_reduce(wave_sum[:], wave[:], AX, ALU.add))
                        V.tensor_scalar(freq[:], wave_sum[:, :, 0], 7.5 / NH, 8.5, ALU.mult, ALU.add)
                        V.tensor_scalar(phase[:], wave_sum[:, :, 1], 16.0 / NH, None, ALU.mult)
                        step_of(V.tensor_scalar(decay[:], wave_sum[:, :, 2], 4.75 / NH, 5.25, ALU.mult, ALU.add))
                        V.reciprocal(rfreq[:], freq[:])
                        V.tensor_tensor(shift[:], centers[:], phase[:], ALU.add)
                        step_of(V.tensor_scalar(decay[:], decay[:], 0.1, None, ALU.max))
                        V.reciprocal(rdecay[:], decay[:])
                        step_of(V.tensor_scalar(shift[:], shift[:], -1.0, 0.5, ALU.mult, ALU.add))
                        V.tensor_tensor(shift2[:], shift[:], rfreq[:], ALU.mult).then_inc(s["geometry"], 1)
                        V.tensor_tensor(freq_decay[:], freq[:], rdecay[:], ALU.mult)
                        V.scalar_tensor_tensor(slopes[:, 0], qk[:], D ** -0.5, over(freq[:], NH), ALU.mult, ALU.mult)
                        step_of(V.tensor_tensor(pos[:], over(freq[:], 2 * MAXK + 1),
                                                strides[:].unsqueeze(1).broadcast_to([P, NT, 2 * MAXK + 1]), ALU.mult))
                        V.tensor_tensor(slopes[:, 1], slopes[:, 0], over(freq_decay[:], NH), ALU.subtract)
                        step_of(V.tensor_tensor(pos[:], pos[:], over(centers[:], 2 * MAXK + 1), ALU.add))
                        step_of(V.tensor_tensor(pos[:], pos[:], over(phase[:], 2 * MAXK + 1), ALU.add))
                        step_of(V.tensor_scalar(valid[:], pos[:], 0.0, None, ALU.is_ge))
                        step_of(V.scalar_tensor_tensor(valid[:].rearrange("p t k -> p (t k)"),
                                                       pos[:].rearrange("p t k -> p (t k)"), float(L),
                                                       valid[:].rearrange("p t k -> p (t k)"),
                                                       ALU.is_lt, ALU.mult))
                        V.tensor_copy(some[:, :, 0:1], valid[:, :, 0:1])
                        step_of(V.tensor_tensor(some[:, :, 1:NK], valid[:, :, 1:NK], valid[:, :, NK:], ALU.add))
                        step_of(V.tensor_scalar(valid[:, :, 0:NK], some[:], 0.0, None, ALU.is_gt))
                        V.tensor_tensor(some2[:], valid[:, :, 0:NK],
                                        strides[:, 0:NK].unsqueeze(1).broadcast_to([P, NT, NK]), ALU.mult)
                        step_of(V.tensor_tensor(valid[:, :, 0:NK], valid[:, :, 0:NK],
                                                falling[:].unsqueeze(1).broadcast_to([P, NT, NK]), ALU.mult))
                        V.tensor_reduce(kmax[:], some2[:], AX, ALU.max)
                        step_of(V.tensor_reduce(kmin[:], valid[:, :, 0:NK], AX, ALU.max))
                        step_of(V.tensor_scalar(kmin[:], kmin[:], -1.0, float(MAXK), ALU.mult, ALU.add))
                        V.tensor_tensor(end1[:], slopes[:, 0], over(kmax[:], NH), ALU.mult)
                        step_of(V.tensor_tensor(end2[:], slopes[:, 0], over(kmin[:], NH), ALU.mult))
                        step_of(V.tensor_tensor(end1[:], end1[:], end2[:], ALU.max))
                        V.tensor_scalar(neg_max[:], end1[:], -1.0, None, ALU.mult).then_inc(s["params"], 1)
                        dve.wait_ge(s["params"], 1)

                    def base(lb):
                        lo, w = window(lb)
                        k = lb % 2
                        dve.wait_ge(s["candidates"], lb + 1)
                        if lb >= 2:
                            dve.wait_ge(s["weight_ready"], NH * (lb - 1))
                            dve.wait_ge(s["hit_turned"], lb - 1)
                        p, d = place[:, k, 0:w], dist[:, k, 0:w]
                        seq(V.tensor_scalar(d.bitcast(U32), samp[:, k, 0:w].bitcast(U32), 0x7FFFFFFF, None,
                                            ALU.bitwise_and))
                        step_of(V.scalar_tensor_tensor(p, p, phase[:, lb:lb + 1], rows[:, lo:lo + w],
                                                       ALU.add, ALU.subtract))
                        V.tensor_scalar(d, d, kmax[:, lb:lb + 1], kmin[:, lb:lb + 1], ALU.min, ALU.max).then_inc(s["dist_ready"], 1)
                        step_of(V.tensor_scalar(not_below[:, 0:w], p, 0.0, None, ALU.is_ge))
                        V.scalar_tensor_tensor(hit[:, k, 0:w], p, 1.0, not_below[:, 0:w], ALU.is_lt, ALU.mult
                                               ).then_inc(s["hit_ready"], 1)

                    def denominators():
                        dve.wait_ge(s["sums_masked"], 1)
                        step_of(V.tensor_reduce(sum_zu[:], sums[:], AX, ALU.add))
                        step_of(V.scalar_tensor_tensor(denom[:], sum_zu[:, 0], 1e-8, sum_zu[:, 1], ALU.mult, ALU.add))
                        seq(V.reciprocal(rdenom[:], denom[:]))

                    def mix_block(lb):
                        dve.wait_ge(s["hit_turned"], lb + 1)
                        ps = misc[:].bitcast(BF16)
                        nf = len(pieces(lb))
                        k = lb % 2
                        if lb >= 3:
                            V.tensor_copy(hitT[0:LOW_ROWS, k, 5, 0:32], tail_hits(0))
                        if lb + 3 < NT:
                            V.tensor_copy(hitT[0:HIGH_ROWS, k, 6, 0:32], tail_hits(1))
                        V.tensor_copy(hitT[:, k, 0:nf, :].rearrange("p c l -> p (c l)"), ps[:, 0:nf * P]
                                      ).then_inc(s["hitT_ready"], 1)
                        dve.wait_ge(s["hitT_ready"], lb + 1)
                        todo = [(hg, sl) for hg in range(2) for sl in slots(lb)]
                        for j, (hg, (kind, c)) in enumerate(todo):
                            n = SLOTS_BEFORE[lb] + j
                            dve.wait_ge(s["turned"], n + 1)
                            if n >= 3:
                                dve.wait_ge(s["mixed_slot"], n - 2)
                            src = turn[n % 2]
                            if kind == "chunk":
                                ins = V.tensor_tensor(weightT[:, n % 3],
                                                      src[:].rearrange("p (g l) -> p g l", g=4),
                                                      hitT[:, k, pieces(lb).index(c), :].unsqueeze(1).broadcast_to([P, 4, P]),
                                                      ALU.mult)
                            else:
                                flat = weightT[:, n % 3].rearrange("p g l -> p (g l)")
                                for ok, r, at, col in ((lb >= 3, LOW_ROWS, 5, 0), (lb + 3 < NT, HIGH_ROWS, 6, P)):
                                    if ok:
                                        ins = V.tensor_tensor(
                                            flat[0:r, col:col + P].rearrange("p (g l) -> p g l", g=4),
                                            src[0:r, col:col + P].rearrange("p (g l) -> p g l", g=4),
                                            hitT[0:r, k, at, 0:32].unsqueeze(1).broadcast_to([r, 4, 32]), ALU.mult)
                            ins.then_inc(s["maskedT"], 1)
                        dve.wait_ge(s["mix_turned"], lb + 1)
                        for par in range(2):
                            src = misc[:, 0:2 * P].rearrange("p (i a) -> p i a", a=64)[:, :, 48 * par:48 * par + D]
                            dst = mix[:, lb].rearrange("p (i q) d -> p i q d", q=2)[:, :, par, :]
                            ins = V.tensor_copy(dst, src)
                        ins.then_inc(s["mix_ready"], 1)

                    def unit(m):
                        hf, e = expert_of(m)
                        dve.wait_ge(s["down_done"], m + 1)
                        if m % (NE + 1):
                            dve.wait_ge(s["acc_done"], m)
                        t0 = hf * NT // 2
                        if e == NE:
                            V.tensor_tensor(acc[:, t0:t0 + NT // 2, :].rearrange("p t c -> p (t c)"), down[m % 2][:],
                                            x1[:, t0:t0 + NT // 2, :].rearrange("p t c -> p (t c)"), ALU.add
                                            ).then_inc(s["acc_done"], 1)
                            return
                        for t in range(NT // 2):
                            a = acc[:, t0 + t, :]
                            ins = V.scalar_tensor_tensor(a, down[m % 2][:, t * C:(t + 1) * C],
                                                         gates[:, t0 + t, e:e + 1], a, ALU.mult, ALU.add)
                        ins.then_inc(s["acc_done"], 1)

                    def post():
                        dve.wait_ge(s["mix_ready"], NT)
                        seq.wait()
                        m3 = mix.rearrange("p t h d -> p (t h) d")
                        V.tensor_tensor(m3, m3, over(rdenom[:], D), ALU.mult).then_inc(s["mix_scaled"], 1)
                        for i, ps in enumerate((misc, mixed)):
                            half = slice(i * HALF, (i + 1) * HALF)
                            dve.wait_ge(s["se1_tanh"], i + 1)
                            step_of(V.tensor_scalar(se_lin[:, half], ps[0:C // 4, :], se1_b[:, 0:1], 0.5,
                                                    ALU.add, ALU.mult))
                            V.scalar_tensor_tensor(se_lin[:, half], se_tanh[:, half], 1.0, se_lin[:, half],
                                                   ALU.add, ALU.mult).then_inc(s["se1_ready"], 1)
                        for i in range(2):
                            half = slice(i * HALF, (i + 1) * HALF)
                            dve.wait_ge(s["se2_tanh"], i + 1)
                            V.scalar_tensor_tensor(xnT[:, half], se_gate[:, half], 1.0, xnT[:, half],
                                                   ALU.add, ALU.mult).then_inc(s["gated"], 1)
                        dve.wait_ge(s["res_loaded"], 16)
                        for i in range(2):
                            half = slice(i * HALF, (i + 1) * HALF)
                            dve.wait_ge(s["out_tanh_ready"], i + 1)
                            step_of(V.scalar_tensor_tensor(attn[:, half], out_tanh[:, half], 1.0, turn[i][:],
                                                           ALU.add, ALU.mult))
                            ins = V.scalar_tensor_tensor(x1[:, 4 * i:4 * i + 4, :].rearrange("p t c -> p (t c)"),
                                                         attn[:, half], 0.5,
                                                         x_res[:, 4 * i:4 * i + 4, :].rearrange("p t c -> p (t c)"),
                                                         ALU.mult, ALU.add)
                        step_of(ins)
                        layernorm(x1, xn2, 2, "xn2_ready")
                        for i in range(2):
                            half = slice(i * HALF, (i + 1) * HALF)
                            dve.wait_ge(s["hi_ready"], i + 1)
                            dve.wait_ge(s["xn2T_ready"], i + 1)
                            V.tensor_tensor(xT_lo[:, half], xn2T[:, half], xT_hi[:, half].bitcast(F32),
                                            ALU.subtract)
                        dve.wait_ge(s["logits_done"], 1)
                        step_of(V.tensor_copy(logits[:].rearrange("p t e -> p (t e)"), misc[:, 0:NT * NE]))
                        for t in range(NT):
                            ins = V.max(out=top[:, t, :], in_=logits[:, t, :])
                        step_of(ins)
                        for t in range(NT):
                            ins = V.max_index(out=top_id[:, t, :], in_max=top[:, t, :], in_values=logits[:, t, :])
                        seq(ins)
                        V.tensor_tensor(gate12[:, 1], top[:, :, 1], top[:, :, 0], ALU.subtract
                                        ).then_inc(s["gap_ready"], 1)
                        seq.wait()
                        V.tensor_copy(top_idf[:], top_id[:])
                        dve.wait_ge(s["gap_exp"], 1)
                        step_of(V.tensor_scalar(gate12[:, 0], gate12[:, 1], 1.0, None, ALU.add))
                        step_of(V.reciprocal(gate12[:, 0], gate12[:, 0]))
                        step_of(V.tensor_tensor(gate12[:, 1], gate12[:, 1], gate12[:, 0], ALU.mult))
                        for i, dst in enumerate((gates, picked)):
                            step_of(V.tensor_tensor(dst[:], expert_ids[:].unsqueeze(1).broadcast_to([P, NT, NE]),
                                                    over(top_idf[:, :, i], NE), ALU.is_equal))
                            step_of(V.tensor_tensor(dst[:], dst[:], over(gate12[:, i], NE), ALU.mult))
                        V.tensor_tensor(gates[:], gates[:], picked[:], ALU.add)

                    for what, n in plan:
                        if what == "prep":
                            prep()
                        elif what == "base":
                            base(n)
                        elif what == "sums":
                            denominators()
                        elif what == "mix":
                            mix_block(n)
                        elif what == "ffn":
                            if n:
                                unit(n - 1)
                        elif what == "post":
                            post()
            clear_semaphores()

        setup()
        clear_semaphores()
        step(0, True, False)
        with nc.Fori(1, B) as b:
            step(b, True, True)
        step(B, False, True)


_INS = ['L0_attn_x', 'L0_attn_w_wave', 'L0_attn_b_wave', 'L0_attn_w_query', 'L0_attn_b_query',
        'L0_attn_key_weight', 'L0_attn_w_se1', 'L0_attn_b_se1', 'L0_attn_w_se2', 'L0_attn_b_se2',
        'L0_attn_w_out', 'L0_ffn_shared_w1', 'L0_ffn_shared_w2', 'L0_ffn_experts_w1',
        'L0_ffn_experts_w2', 'L0_ffn_gate_w']


def kernel(**inputs):
    import numpy as np
    import concourse.bacc as bacc
    from concourse.bass_utils import run_bass_kernel_spmd

    nc = bacc.Bacc("TRN2", target_bir_lowering=False, num_devices=1)
    arrays, args = {}, []
    for name in _INS:
        a = np.ascontiguousarray(inputs[name])
        arrays[f"in_{name}"] = a
        args.append(nc.dram_tensor(f"in_{name}", a.shape, mybir.dt.from_np(a.dtype), kind="ExternalInput").ap())
    shape = inputs['L0_attn_x'].shape
    result = nc.dram_tensor("out_x", shape, mybir.dt.float32, kind="ExternalOutput").ap()
    build_program(nc, *args, result)
    r = run_bass_kernel_spmd(nc, [arrays], core_ids=[0])
    return r.results[0]["out_x"]
```

```python
from contextlib import ExitStack

import concourse.bass as bass
from concourse import mybir


def build_program(nc, x, w_wave, b_wave, w_query, b_query, key_weight, w_se1, b_se1, w_se2, b_se2,
                  w_out, shared_w1, shared_w2, experts_w1, experts_w2, gate_w, out):
    F32, F32R, BF16 = mybir.dt.float32, mybir.dt.float32r, mybir.dt.bfloat16
    U32 = mybir.dt.uint32
    ALU = mybir.AluOpType
    ACT = mybir.ActivationFunctionType
    AX = mybir.AxisListType.X

    P = 128
    B, L, C = x.shape
    NT = L // P
    NH = w_wave.shape[1] // 3
    D = C // NH
    NW, NQ = w_wave.shape[1], w_query.shape[1]
    NP = NW + NQ
    MAXK = 16
    NK = MAXK + 1
    NE = experts_w1.shape[0]
    HID = experts_w1.shape[1]
    NHC = HID // P
    HALF = L // 2
    EPS = 1e-5
    LOW, HIGH = 264, 336
    MAGIC = float(3 * 2 ** 22)
    NU = 2 * (NE + 1)

    HB = P // 2
    NJ = L // HB

    def window(j):
        first, end = j * HB - LOW, j * HB + HIGH
        if first < 0:
            return 0, 0, 0, -(-end // P)
        if end > L:
            c = first // P
            return 0, c, c * P, NT - c
        copy = 1 if first % P == SHIFTS[1] else 2
        return copy, first // P, first, -(-(end - first) // P)

    SHIFTS = (0, (-LOW) % P, (HB - LOW) % P)
    SLOTS = [(j, i) for j in range(NJ) for i in range(window(j)[3])]
    SLOTS_BEFORE = [sum(window(k)[3] for k in range(j)) for j in range(NJ + 1)]
    NS = len(SLOTS)
    WMAX = P * max(window(j)[3] for j in range(NJ))
    MISS = -256.0
    UNITS_AFTER = (2, 2, 2, 2, 2, 2, 2, 1)
    NX, NWT = 2, 3

    ctx = ExitStack()
    with ctx:
        def sb(name, shape, dt=F32):
            return ctx.enter_context(nc.sbuf_tensor(name, shape, dt))

        def sem(name):
            return ctx.enter_context(nc.semaphore(name))

        ident = sb("ident", [P, P])
        ident_bf = sb("ident_bf", [P, P], BF16)
        rows = sb("rows", [P, L])
        half_ident = sb("half_ident", [P, HB])
        pick = sb("pick", [P, 2, P])
        parity = sb("parity", [P, 2])
        strides = sb("strides", [P, 2 * MAXK + 1])
        falling = sb("falling", [P, NK])
        minus_half = sb("minus_half", [P, 2, NT])
        expert_ids = sb("expert_ids", [P, NE])
        w_proj = sb("w_proj", [P, NP])
        bias_proj = sb("bias_proj", [P, NP])
        key_w = sb("key_w", [P, NH, D])
        se1_w = sb("se1_w", [P, C // 4])
        se2_w = sb("se2_w", [C // 4, C])
        se1_b = sb("se1_b", [C // 4, 2])
        se2_b = sb("se2_b", [C, 2])
        out_w = sb("out_w", [P, C])
        gate_raw = sb("gate_raw", [NE, C])
        gate_wT = sb("gate_wT", [P, NE])
        w1_hi = sb("w1_hi", [P, NE + 1, HID], F32R)
        w1_lo = sb("w1_lo", [P, NE + 1, HID], F32R)
        w2T = sb("w2T", [P, NE + 1, NHC, C])

        x_in = sb("x_in", [P, NT, C])
        x_res = sb("x_res", [P, NT, C])
        xn = sb("xn", [P, NT, C])
        xnT = sb("xnT", [P, L])
        stats = sb("stats", [P, 2, NT, 6])
        mean_var = sb("mean_var", [P, 2, NT, 2])
        var_eps = sb("var_eps", [P, 2, NT])
        rstd = sb("rstd", [P, 2, NT])
        wave = sb("wave", [P, NT, 3, NH])
        wave_sum = sb("wave_sum", [P, NT, 3])
        decay = sb("decay", [P, NT])
        rdecay = sb("rdecay", [P, NT])
        freq_decay = sb("freq_decay", [P, NT])
        shift = sb("shift", [P, NT])
        qk = sb("qk", [P, NT, NH])
        slope_s = sb("slope_s", [P, NT, NH])
        token = sb("token", [P, 7 * NT + NT * NH])
        freq, phase, centers, rfreq, shift2, kmax, kmin = (token[:, i * NT:(i + 1) * NT] for i in range(7))
        slope_e = token[:, 7 * NT:].rearrange("p (t h) -> p t h", h=NH)
        twice = sb("twice", [P, 2, 7 * NT])
        slope_parts = sb("slope_parts", [P, 2, NT * NH], F32R)
        max_parts = sb("max_parts", [NT * NH, 2, P], F32R)
        end1 = sb("end1", [P, NT, NH])
        end2 = sb("end2", [P, NT, NH])
        neg_max = sb("neg_max", [P, NT, NH])
        pos = sb("pos", [P, NT, 2 * MAXK + 1])
        valid = sb("valid", [P, NT, 2 * MAXK + 1])
        some = sb("some", [P, NT, NK])
        some2 = sb("some2", [P, NT, NK])
        kept = some2
        sums = sb("sums", [P, 2, NT * NH, NK])
        half_tanh = sums[:].rearrange("p a n k -> p (a n k)")[:, 0:NT * NP].rearrange("p (t n) -> p t n", t=NT)
        sum_zu = sb("sum_zu", [P, 2, NT * NH])
        denom = sb("denom", [P, NT * NH])
        rdenom = sb("rdenom", [P, NT * NH])

        samp = sb("samp", [P, 2, WMAX])
        place = sb("place", [P, 2, WMAX])
        above = sb("above", [HB, WMAX])
        dist = sb("dist", [P, 2, WMAX], F32R)
        miss = sb("miss", [HB + 2, 2, WMAX], F32R)
        slope_diag = sb("slope_diag", [P, 2, NH, HB], F32R)
        miss_diag = sb("miss_diag", [HB + 2, 2, NH, P], F32R)
        weightT = sb("weightT", [P, NWT, NH * HB])

        x1 = sb("x1", [P, NT, C])
        acc = sb("acc", [P, NT, C])
        xT_hi = sb("xT_hi", [P, L], F32R)
        xT_lo = sb("xT_lo", [P, L], F32R)
        hidden = sb("hidden", [P, 2, NHC, HALF])
        gates = sb("gates", [P, NT, NE])
        logits = sb("logits", [P, NT, NE])
        top = sb("top", [P, NT, 8])
        top_id = sb("top_id", [P, NT, 8], U32)
        top_idf = end2
        gap = sb("gap", [P, NT])
        gate12 = sb("gate12", [P, 2, NT])
        picked = logits

        shared = sb("shared", [P, 2 * (NE + 1) * HID])
        raw_w1 = shared[:, 0:(NE + 1) * HID].rearrange("p (e k d) -> p e k d", e=NE + 1, d=C)
        raw_w2 = shared[:, (NE + 1) * HID:].rearrange("p (e h) -> p e h", e=NE + 1)
        moved = shared[:, 0:2 * (NT - 1) * C].rearrange("p (a t c) -> p a t c", a=2, c=C)
        proj = shared[:, 5 * L:5 * L + NT * NP].rearrange("p (t n) -> p t n", t=NT)
        se_tanh, se_lin = shared[0:C // 4, 0:L], shared[0:C // 4, L:2 * L]
        se_gate, out_tanh, attn = shared[:, 2 * L:3 * L], shared[:, 3 * L:4 * L], shared[:, 4 * L:5 * L]
        xn2 = shared[:, 5 * L:6 * L].rearrange("p (t c) -> p t c", t=NT)
        xn2T = shared[:, 6 * L:7 * L]
        next_xT = shared[:, 8 * L:9 * L]
        rdenom_wide = shared[:, 7 * L:8 * L].rearrange("p (n d) -> p n d", d=D)

        bank = [ctx.enter_context(nc.psum_tensor(f"bank{i}", [P, 512], F32)) for i in range(8)]
        turn = bank[0:NX]
        ahead_ps = bank[2]
        mixed = bank[3:5]
        misc = bank[4]
        up = bank[5:7]

        down = bank[7]
        NG = 5 * NT
        NR = 2 * NT + NT * NH
        MAX_AT = 2 * NG + 2 * NR

        names = ("setup_consts setup_act setup_dve raw_loaded small_loaded gate_turned "
                 "weights_turned weights_hi weights_free "
                 "x_loaded res_loaded var2_ready rstd2_ready var_ready rstd_ready xn_ready x_ready rows_moved xn_turned xnT_ready "
                 "proj_done proj_ready tanh_ready silu_ready wave_ready geometry geometry_twice "
                 "geometry_out params params_twice params_out max_ready max_rows_even max_rows_odd sums_ready "
                 "sums_exp sums_masked wide_ready candidates window_ready slopes_ready "
                 "first_candidates first_windows first_rows "
                 "exponents weights_ready mixed_slot gathered "
                 "rdenom_turned mix_ready se1_done se1_tanh se1_ready se2_done se2_tanh "
                 "gated out_done out_tanh_ready x1_ready xn2_ready xn2_turned xn2T_ready hi_ready lo_ready "
                 "logits_done logits_read gap_ready gap_tanh up_done silu_done down_done acc_done stored "
                 "dve_seq pool_seq").split()
        s = {n: sem(n) for n in names}
        max_rows = (s["max_rows_even"], s["max_rows_odd"])

        x_dram = x.rearrange("b (t p) c -> p (b t) c", p=P)
        out_dram = out.rearrange("b (t p) c -> p (b t) c", p=P)

        class Chain:

            def __init__(self, eng, sem):
                self.eng, self.sem, self.n = eng, sem, 0

            def __call__(self, ins):
                self.n += 1
                ins.then_inc(self.sem, 1)

            def wait(self):
                self.eng.wait_ge(self.sem, self.n)

        def clear_semaphores():
            with nc.Block(no_gpsimd_drain=True) as block:
                @block.sync
                def _(sp):
                    for n in names[0::5]:
                        sp.sem_clear(s[n])

                @block.gpsimd
                def _(pool):
                    for n in names[1::5]:
                        pool.sem_clear(s[n])

                @block.scalar
                def _(act):
                    for n in names[2::5]:
                        act.sem_clear(s[n])

                @block.vector
                def _(dve):
                    for n in names[3::5]:
                        dve.sem_clear(s[n])

                @block.tensor
                def _(pe):
                    for n in names[4::5]:
                        pe.sem_clear(s[n])

        def setup():
            with nc.Block() as block:
                @block.sync
                def _(sp):
                    sp.dma_start(x_in[:], x_dram[:, 0:NT, :]).then_inc(s["x_loaded"], 16)
                    for e in range(NE):
                        sp.dma_start(raw_w1[:, e], experts_w1[e].rearrange("(k p) d -> p k d", p=P)
                                     ).then_inc(s["raw_loaded"], 16)
                    sp.dma_start(raw_w1[:, NE], shared_w1.rearrange("(k p) d -> p k d", p=P)
                                 ).then_inc(s["raw_loaded"], 16)
                    sp.dma_start(raw_w2[:, 0:NE], experts_w2.rearrange("e d h -> d e h")
                                 ).then_inc(s["raw_loaded"], 16)
                    sp.dma_start(raw_w2[:, NE], shared_w2).then_inc(s["raw_loaded"], 16)
                    sp.wait_ge(s["x_loaded"], 16)

                @block.gpsimd
                def _(pool):
                    seq = Chain(pool, s["pool_seq"])
                    nc.gpsimd.memset(ident[:], 0.0)
                    seq(nc.gpsimd.memset(ident_bf[:], 0.0))
                    seq.wait()
                    for m in (ident, ident_bf):
                        nc.gpsimd.affine_select(out=m[:], in_=m[:], compare_op=ALU.not_equal, fill=1.0,
                                                base=0, pattern=[[-1, P]], channel_multiplier=1)
                    nc.gpsimd.memset(minus_half[:], -0.5)
                    iota = dict(allow_small_or_imprecise_dtypes=True)
                    nc.gpsimd.iota(rows[:], [[1, L]], base=0, channel_multiplier=0, **iota)
                    nc.gpsimd.iota(centers, [[P, NT]], base=0, channel_multiplier=1, **iota)
                    nc.gpsimd.iota(strides[:, 0:NK], [[1, NK]], base=0, channel_multiplier=0, **iota)
                    nc.gpsimd.iota(strides[:, NK:], [[-1, MAXK]], base=-1, channel_multiplier=0, **iota)
                    nc.gpsimd.iota(falling[:], [[-1, NK]], base=MAXK, channel_multiplier=0, **iota)
                    nc.gpsimd.iota(expert_ids[:], [[1, NE]], base=0, channel_multiplier=0,
                                   **iota).then_inc(s["setup_consts"], 1)

                @block.scalar
                def _(act):
                    small = [(w_proj[:, 0:NW], w_wave), (w_proj[:, NW:NP], w_query),
                             (bias_proj[:, 0:NW], b_wave.partition_broadcast(P)),
                             (bias_proj[:, NW:NP], b_query.partition_broadcast(P)),
                             (key_w[:, 0, :], key_weight.partition_broadcast(P)),
                             (se1_w[:], w_se1), (se2_w[:], w_se2),
                             (se1_b[:, 0:1], b_se1.rearrange("(p a) -> p a", a=1)),
                             (se2_b[:, 0:1], b_se2.rearrange("(p a) -> p a", a=1)),
                             (out_w[:], w_out), (gate_raw[:], gate_w)]
                    for dst, src in small:
                        act.dma_start(dst, src).then_inc(s["small_loaded"], 16)
                    for g in range(2 * (NE + 1)):
                        act.wait_ge(s["weights_turned"], g + 1)
                        e = g % (NE + 1)
                        dst = w1_hi[:, e, :] if g <= NE else w2T[:, e].rearrange("p k d -> p (k d)")
                        nc.scalar.activation(dst, turn[g % 2][:], ACT.Copy).then_inc(s["weights_hi"], 1)
                    act.wait_ge(s["gate_turned"], 1)
                    nc.scalar.activation(gate_wT[:], misc[:, 0:NE], ACT.Copy)

                @block.tensor
                def _(pe):
                    pe.wait_ge(s["setup_consts"], 1)
                    pe.wait_ge(s["raw_loaded"], 16 * (NE + 3))
                    for g in range(2 * (NE + 1)):
                        e = g % (NE + 1)
                        if g >= 2:
                            pe.wait_ge(s["weights_hi"], g - 1)
                            pe.wait_ge(s["weights_free"], min(g - 1, NE + 1))
                        for k in range(NHC):
                            src = raw_w1[:, e, k, :] if g <= NE else raw_w2[:, e, k * P:(k + 1) * P]
                            ins = nc.tensor.transpose(turn[g % 2][:, k * P:(k + 1) * P], src, ident[:])
                        ins.then_inc(s["weights_turned"], 1)
                    pe.wait_ge(s["small_loaded"], 16 * 11)
                    nc.tensor.transpose(misc[:, 0:NE], gate_raw[:], ident[0:NE, 0:NE]
                                        ).then_inc(s["gate_turned"], 1)

                @block.vector
                def _(dve):
                    for g in range(NE + 1):
                        dve.wait_ge(s["weights_hi"], g + 1)
                        nc.vector.tensor_tensor(w1_lo[:, g, :], turn[g % 2][:],
                                                w1_hi[:, g, :].bitcast(F32), ALU.subtract
                                                ).then_inc(s["weights_free"], 1)
                    dve.wait_ge(s["setup_consts"], 1)
                    for hf in range(2):
                        for i in range(2):
                            nc.vector.tensor_copy(pick[:, hf, i * HB:(i + 1) * HB], ident[:, hf * HB:(hf + 1) * HB])
                    nc.vector.tensor_tensor(half_ident[:], ident[:, 0:HB], ident[:, HB:P], ALU.add)
                    nc.vector.tensor_reduce(stats[:, 0, 0:2, 0:4], ident[:].rearrange(
                        "p (g q d) -> p q g d", q=2, d=D), AX, ALU.add).then_inc(s["dve_seq"], 1)
                    dve.wait_ge(s["dve_seq"], 1)
                    nc.vector.tensor_reduce(parity[:], stats[:, 0, 0:2, 0:4], AX, ALU.add)
                    for r in range(2):
                        for h in range(NH):
                            for i in range(2):
                                nc.vector.tensor_scalar(miss_diag[0:HB, r, h, i * HB:(i + 1) * HB],
                                                        ident[0:HB, 0:HB], MISS, None, ALU.mult)
                    for k in range(2):
                        nc.vector.tensor_scalar(miss[HB:HB + 2, k, :], rows[HB:HB + 2, 0:WMAX], 0.0, 1.0,
                                                ALU.mult, ALU.add)
                    dve.wait_ge(s["small_loaded"], 16 * 11)
                    for h in range(1, NH):
                        nc.vector.tensor_copy(key_w[:, h, :], key_w[:, 0, :])
                    nc.vector.tensor_scalar(se1_b[:, 1:2], se1_b[:, 0:1], 0.5, None, ALU.mult)
                    nc.vector.tensor_scalar(se2_b[:, 1:2], se2_b[:, 0:1], 0.5, None, ALU.mult)
                    nc.vector.tensor_scalar(out_w[:], out_w[:], 0.5, None, ALU.mult)

        def step(b, attention, ffn, ahead):
            plan = []
            units = [([("up", m * NHC + k) for k in range(NHC)] if m < NU else []) +
                     ([("down", m - 1)] if m else []) for m in range(NU + 1)] if ffn else []

            def ffn_units(n):
                for _ in range(n):
                    plan.extend(units.pop(0) if units else [])

            def begin(n):
                plan.extend([("exponent", n), ("exp", n)])

            behind = {j: [("base", j + 2), ("slopes", j + 2)] for j in range(NJ - 2)}
            behind.update({j: [] for j in range(NJ - 2, NJ)})
            behind[0] = [("ffn norm", 1)] + behind[0]
            behind[1] = [("ffn head", 0)] + behind[1] + [("ffn head", 1)]
            behind[2] += [("ffn head", 2), ("ffn head", 3)]
            for j, k in ((4, 0), (5, 1), (6, 2), (7, 3), (8, 4), (9, 5), (10, 6), (11, 7)):
                behind[j] += [("sums", k)]
            if ahead:
                behind[4] += [("ahead root", 0)]
                for j, k in ((3, 0), (5, 1), (6, 2), (7, 3), (8, 4), (9, 5), (10, 6), (12, 7), (13, 8), (14, 9)):
                    behind[j] += [("ahead", k)]

            plan.append(("ffn norm", 0))
            if attention:
                begun = 0
                for t in range(NT):
                    for n in range(SLOTS_BEFORE[2 * t], SLOTS_BEFORE[2 * t + 2]):
                        if n >= begun:
                            begin(n)
                            begun = n + 1
                        if n - NX >= SLOTS_BEFORE[2 * t]:
                            plan.append(("product", n - NX))
                        j, i = SLOTS[n]
                        if i == window(j)[3] - 1:
                            plan += behind[j]
                    last = SLOTS_BEFORE[2 * t + 2] - 1
                    count = UNITS_AFTER[t]
                    unit = units.pop(0) if units and count else []
                    plan += unit[0:1] + [("product", last - 1)] + unit[1:2] + [("product", last)]
                    if count > 1:
                        plan += unit[NHC:] + unit[2:NHC]
                        ffn_units(count - 2)
                        unit = units.pop(0) if units else []
                        plan += unit[0:NHC]
                    else:
                        plan += unit[2:NHC]
                    plan.append(("gather", t))
                    if t + 1 < NT:
                        for n in range(last + 1, last + 1 + NX):
                            begin(n)
                            begun = n + 1
                    plan += unit[NHC:]
                for k in range(4):
                    plan.append(("post", k))
                    if k < 3:
                        ffn_units(1)
                    if k < 2 and ahead:
                        plan.append(("ahead", 10 + k))
            else:
                plan += [("ffn norm", 1), ("ffn head", 0), ("ffn head", 1), ("ffn head", 2), ("ffn head", 3)]
                if ahead:
                    plan.append(("ahead root", 0))
                    plan += [("ahead", k) for k in range(12)]
            ffn_units(len(units))
            if not ffn:
                plan = [item for item in plan if not item[0].startswith("ffn")]
            if not attention:
                plan = [item for item in plan if item[0] != "sums"]

            def expert_of(m):
                return m // (NE + 1), (m - 1) % (NE + 1) if m % (NE + 1) else NE

            with nc.Block(no_gpsimd_drain=True) as block:

                @block.sync
                def _(sp):
                    def load_max_rows(t, done):
                        for part in range(2):
                            sp.dma_start(miss_diag[HB + part:HB + part + 1, t % 2].bitcast(F32),
                                         max_parts[t * NH:(t + 1) * NH, part, :].bitcast(F32)).then_inc(done, 16)

                    def store(hf):
                        sp.dma_start(out_dram[:, bass.ds((b - 1) * NT + hf * NT // 2, NT // 2), :],
                                     acc[:, hf * NT // 2:(hf + 1) * NT // 2]).then_inc(s["stored"], 16)

                    if attention:
                        sp.dma_start(x_res[:], x_dram[:, bass.ds(b * NT, NT), :]).then_inc(s["res_loaded"], 16)
                        for a in range(2):
                            r = SHIFTS[a + 1]
                            sp.dma_start(moved[0:P - r, a], xn[r:P, 0:NT - 1]).then_inc(s["rows_moved"], 16)
                            sp.dma_start(moved[P - r:P, a], xn[0:r, 1:NT]).then_inc(s["rows_moved"], 16)
                        if ahead:
                            sp.dma_start(x_in[:], x_dram[:, bass.ds((b + 1) % B * NT, NT), :]
                                         ).then_inc(s["x_loaded"], 16)
                        for t in range(2, NT):
                            sp.wait_ge(s["exponents"], SLOTS_BEFORE[2 * t - 2])
                            load_max_rows(t, max_rows[t % 2])
                    if ffn:
                        sp.wait_ge(s["acc_done"], NE + 1)
                        store(0)
                    if ahead:
                        sp.wait_ge(s["max_ready"], 1)
                        for t in range(2):
                            load_max_rows(t, s["first_rows"])
                    if ffn:
                        sp.wait_ge(s["acc_done"], 2 * (NE + 1))
                        store(1)
                        sp.wait_ge(s["stored"], 32)
                    if attention:
                        sp.wait_ge(max_rows[0], 16 * (NT - 2))
                        sp.wait_ge(max_rows[1], 16 * (NT - 2))
                        sp.wait_ge(s["rows_moved"], 64)
                        sp.wait_ge(s["res_loaded"], 16)
                    if ahead:
                        sp.wait_ge(s["first_rows"], 64)
                        if attention:
                            sp.wait_ge(s["x_loaded"], 16)

                @block.gpsimd
                def _(pool):
                    seq = Chain(pool, s["pool_seq"])

                    def reciprocal_root(a):
                        pool.wait_ge(s[("var_ready", "var2_ready")[a]], 1)
                        nc.gpsimd.tensor_tensor(rstd[:, a], var_eps[:, a], minus_half[:, a], ALU.pow
                                                ).then_inc(s[("rstd_ready", "rstd2_ready")[a]], 1)

                    def base(j, first=False):
                        _, _, lo, chunks = window(j)
                        w = chunks * P
                        k = j % 2
                        of = twice[:, k].rearrange("p (i t) -> p i t", t=NT)[:, :, j // 2:j // 2 + 1]
                        if first:
                            pool.wait_ge(s["geometry_out"], 1)
                            if attention:
                                pool.wait_ge(s["window_ready"], NJ - 2)
                        elif j >= 4:
                            pool.wait_ge(s["window_ready"], j - 3)
                        r = samp[:, k, 0:w]
                        seq(nc.gpsimd.tensor_scalar(r, rows[:, lo:lo + w], of[:, 3], of[:, 4], ALU.mult, ALU.add))
                        seq.wait()
                        seq(nc.gpsimd.tensor_scalar(r, r, MAGIC, MAGIC - MAXK, ALU.add, ALU.max))
                        seq.wait()
                        seq(nc.gpsimd.tensor_scalar(r, r, MAGIC + MAXK, MAGIC, ALU.min, ALU.subtract))
                        seq.wait()
                        nc.gpsimd.tensor_scalar(place[:, k, 0:w], r, of[:, 0], of[:, 2], ALU.mult, ALU.add
                                                ).then_inc(s["first_candidates" if first else "candidates"], 1)

                    def terms(part):
                        a = part % 2
                        v = sums[:, a].rearrange("p (t h) k -> p t h k", t=NT)
                        if part < 2:
                            seq(nc.gpsimd.tensor_tensor(
                                v, (slope_s[:], slope_e)[a].unsqueeze(3).broadcast_to([P, NT, NH, NK]),
                                kept[:].unsqueeze(2).broadcast_to([P, NT, NH, NK]), ALU.mult))
                        elif part < 4:
                            seq.wait()
                            nc.gpsimd.tensor_tensor(
                                v, v, neg_max[:].unsqueeze(3).broadcast_to([P, NT, NH, NK]), ALU.add
                                ).then_inc(s["sums_ready"], 1)
                        else:
                            pool.wait_ge(s["sums_exp"], 1)
                            nc.gpsimd.tensor_tensor(
                                v, v, some[:].unsqueeze(2).broadcast_to([P, NT, NH, NK]), ALU.mult
                                ).then_inc(s["sums_masked"], 1)

                    for what, n in plan:
                        if what == "ffn norm" and n == 0:
                            reciprocal_root(1)
                        elif what == "ahead root":
                            reciprocal_root(0)
                        elif what == "ahead" and n == 11:
                            base(0, first=True)
                            base(1, first=True)
                        elif what == "base":
                            base(n)
                        elif what == "sums" and n != 4 and n != 7:
                            terms(n if n < 4 else n - 1)

                @block.scalar
                def _(act):
                    def copy(dst, src):
                        return nc.scalar.activation(dst, src, ACT.Copy)

                    def ffn_head():
                        for i in range(2):
                            act.wait_ge(s["xn2_turned"], i + 1)
                            copy(xT_hi[:, i * HALF:(i + 1) * HALF], up[i][:]).then_inc(s["hi_ready"], 1)
                            copy(xn2T[:, i * HALF:(i + 1) * HALF], up[i][:]).then_inc(s["xn2T_ready"], 1)

                    def gap_tanh():
                        act.wait_ge(s["gap_ready"], 1)
                        nc.scalar.activation(gap[:], gap[:], ACT.Tanh, scale=0.5).then_inc(s["gap_tanh"], 1)

                    def prepare(part):
                        if part in (2, 3):
                            i = part - 2
                            act.wait_ge(s["xn_turned"], i + 1)
                            copy(next_xT[:, i * HALF:(i + 1) * HALF], ahead_ps[:]).then_inc(s["xnT_ready"], 1)
                        elif part == 7:
                            act.wait_ge(s["proj_ready"], 3)
                            if attention:
                                act.wait_ge(s["wide_ready"], 1)
                            nc.scalar.activation(half_tanh, proj, ACT.Tanh, scale=0.5
                                                 ).then_inc(s["tanh_ready"], 1)
                        elif part == 11:
                            if attention:
                                act.wait_ge(s["mixed_slot"], NS)
                            act.wait_ge(s["x_ready"], 1)
                            copy(xn[:], x_in[:])
                        elif part == 8:
                            act.wait_ge(s["silu_ready"], 1)
                            wv = proj[:, :, 0:NW].rearrange("p t (k h) -> p t k h", k=3)
                            nc.scalar.activation(wave[:, :, 0:3:2, :], wv[:, :, 0:3:2, :], ACT.Tanh, scale=0.5)
                            nc.scalar.activation(wave[:, :, 1, :], wv[:, :, 1, :], ACT.Tanh
                                                 ).then_inc(s["wave_ready"], 1)

                    def exps(n):
                        act.wait_ge(s["exponents"], n + 1)
                        if n >= NWT:
                            act.wait_ge(s["mixed_slot"], n - NWT + 1)
                        nc.scalar.activation(weightT[:, n % NWT], turn[n % NX][:], ACT.Exp
                                             ).then_inc(s["weights_ready"], 1)

                    def sums_exp():
                        act.wait_ge(s["sums_ready"], 2)
                        flat = sums[:].rearrange("p a n k -> p (a n k)")
                        nc.scalar.activation(flat, flat, ACT.Exp).then_inc(s["sums_exp"], 1)

                    def unit(n):
                        m, k = n // NHC, n % NHC
                        if m >= 2 and k == 0:
                            act.wait_ge(s["down_done"], m - 1)
                        act.wait_ge(s["up_done"], n + 1)
                        nc.scalar.activation(hidden[:, m % 2, k, :], up[n % 2][:], ACT.Silu
                                             ).then_inc(s["silu_done"], 1)

                    def post(part):
                        for i in range(2):
                            half = slice(i * HALF, (i + 1) * HALF)
                            if part == 1:
                                act.wait_ge(s["se1_done"], i + 1)
                                nc.scalar.activation(se_tanh[:, half], mixed[i][0:C // 4, :], ACT.Tanh,
                                                     scale=0.5, bias=se1_b[:, 1:2]).then_inc(s["se1_tanh"], 1)
                            elif part == 2:
                                act.wait_ge(s["se2_done"], i + 1)
                                nc.scalar.activation(se_gate[:, half], turn[i][:], ACT.Tanh,
                                                     scale=0.5, bias=se2_b[:, 1:2]).then_inc(s["se2_tanh"], 1)
                            elif part == 3:
                                act.wait_ge(s["out_done"], i + 1)
                                nc.scalar.activation(out_tanh[:, half], turn[i][:], ACT.Tanh,
                                                     scale=0.5).then_inc(s["out_tanh_ready"], 1)

                    for what, n in plan:
                        if what == "ffn head" and n == 0:
                            ffn_head()
                        elif what == "ffn head" and n == 2:
                            gap_tanh()
                        elif what == "ahead":
                            prepare(n)
                        elif what == "exp":
                            exps(n)
                        elif what == "sums" and n == 4:
                            sums_exp()
                        elif what == "up":
                            unit(n)
                        elif what == "post":
                            post(n)

                @block.tensor
                def _(pe):
                    def turn_all(src, banks, signal):
                        for i, ps in enumerate(banks):
                            turn_four(lambda t: src(4 * i + t), ps, signal)

                    def turn_four(src, ps, signal):
                        for t in range(4):
                            ins = nc.tensor.transpose(ps[:, t * P:(t + 1) * P], src(t), ident[:])
                        ins.then_inc(s[signal], 1)

                    def ffn_turn():
                        pe.wait_ge(s["xn2_ready"], 1)
                        turn_all(lambda t: xn2[:, t, :], up, "xn2_turned")

                    def ffn_logits():
                        pe.wait_ge(s["xn2T_ready"], 2)
                        for t in range(NT):
                            ins = nc.tensor.matmul(down[:, t * NE:(t + 1) * NE], xn2T[:, t * P:(t + 1) * P],
                                                   gate_wT[:], start=True, stop=True)
                        ins.then_inc(s["logits_done"], 1)

                    def prepare(part):
                        if part in (2, 3):
                            i = part - 2
                            pe.wait_ge(s["x_ready"], 1)
                            if i:
                                pe.wait_ge(s["xnT_ready"], 1)
                            turn_four(lambda t: x_in[:, 4 * i + t, :], ahead_ps, "xn_turned")
                        elif part in (4, 5, 6):
                            g = part - 4
                            if g == 0:
                                pe.wait_ge(s["xnT_ready"], 2)
                            else:
                                pe.wait_ge(s["proj_ready"], g)
                            for t in range(3 * g, min(3 * g + 3, NT)):
                                ins = nc.tensor.matmul(ahead_ps[:, (t - 3 * g) * NP:(t - 3 * g + 1) * NP],
                                                       next_xT[:, t * P:(t + 1) * P], w_proj[:], start=True, stop=True)
                            ins.then_inc(s["proj_done"], 1)
                        elif part == 9:
                            geometry_twice()
                        elif part == 10:
                            params_twice()

                    def geometry_twice():
                        pe.wait_ge(s["geometry"], 1)
                        pe.wait_ge(s["proj_ready"], 3)
                        for hf in range(2):
                            ins = nc.tensor.matmul(ahead_ps[:, hf * NG:(hf + 1) * NG], pick[:, hf, :], token[:, 0:NG],
                                                   start=True, stop=True)
                        ins.then_inc(s["geometry_twice"], 1)

                    def params_twice():
                        pe.wait_ge(s["params"], 1)
                        pe.wait_ge(s["geometry_out"], 1)
                        for hf in range(2):
                            nc.tensor.matmul(ahead_ps[:, 2 * NG + hf * NR:2 * NG + (hf + 1) * NR], pick[:, hf, :],
                                             token[:, NG:NG + NR], start=True, stop=True)
                        nc.tensor.transpose(ahead_ps[0:NT * NH, MAX_AT:MAX_AT + P],
                                            neg_max[:].rearrange("p t h -> p (t h)"), ident[:]
                                            ).then_inc(s["params_twice"], 1)

                    def exponent(n):
                        j, i = SLOTS[n]
                        k = j % 2
                        if i == 0 and j >= 2:
                            pe.wait_ge(s["window_ready"], j - 1)
                            pe.wait_ge(s["slopes_ready"], j - 1)
                        if i == 0 and j >= 4:
                            pe.wait_ge(max_rows[j // 2 % 2], 32 * (j // 4))
                        if n >= NX:
                            pe.wait_ge(s["weights_ready"], n - NX + 1)
                        cols = slice(i * P, (i + 1) * P)
                        nc.tensor.matmul(turn[n % NX][:], dist[:, k, cols],
                                         slope_diag[:, k].rearrange("p h l -> p (h l)"), start=True, stop=False)
                        nc.tensor.matmul(turn[n % NX][:], miss[:, k, cols],
                                         miss_diag[:, j // 2 % 2, :, k * HB:(k + 1) * HB], start=False, stop=True
                                         ).then_inc(s["exponents"], 1)

                    def product(n):
                        j, i = SLOTS[n]
                        copy, c0, _, chunks = window(j)
                        pe.wait_ge(s["weights_ready"], n + 1)
                        if copy and i == 0:
                            pe.wait_ge(s["rows_moved"], 64)
                        if i == 0 and j >= 4:
                            pe.wait_ge(s["gathered"], j // 2 - 1)
                        rows_of = xn[:, c0 + i, :] if copy == 0 else moved[:, copy - 1, c0 + i, :]
                        for g in range(4):
                            ins = nc.tensor.matmul(mixed[j // 2 % 2][32 * g:32 * g + 32, j % 2 * P:(j % 2 + 1) * P],
                                                   rows_of[:, 32 * g:32 * g + 32], weightT[:, n % NWT, g * P:(g + 1) * P],
                                                   start=i == 0, stop=i == chunks - 1)
                        ins.then_inc(s["mixed_slot"], 1)

                    def unit_up(n):
                        m, k = n // NHC, n % NHC
                        hf, e = expert_of(m)
                        cols = slice(hf * HALF, (hf + 1) * HALF)
                        if k == 0 and m % (NE + 1) == 0:
                            pe.wait_ge(s["hi_ready"], 2)
                            pe.wait_ge(s["lo_ready"], 2)
                        if n >= 2:
                            pe.wait_ge(s["silu_done"], n - 1)
                        hs = slice(k * P, (k + 1) * P)
                        nc.tensor.matmul(up[n % 2][:], w1_hi[:, e, hs], xT_hi[:, cols], start=True, stop=False)
                        nc.tensor.matmul(up[n % 2][:], w1_hi[:, e, hs], xT_lo[:, cols], start=False, stop=False)
                        nc.tensor.matmul(up[n % 2][:], w1_lo[:, e, hs], xT_hi[:, cols], start=False, stop=True
                                         ).then_inc(s["up_done"], 1)

                    def unit_down(m):
                        _, e = expert_of(m)
                        pe.wait_ge(s["silu_done"], NHC * (m + 1))
                        if m == 0:
                            pe.wait_ge(s["logits_read"], 1)
                        if m:
                            pe.wait_ge(s["acc_done"], m)
                        for t in range(NT // 2):
                            for k in range(NHC):
                                ins = nc.tensor.matmul(down[:, t * C:(t + 1) * C],
                                                       hidden[:, m % 2, k, t * P:(t + 1) * P], w2T[:, e, k, :],
                                                       start=k == 0, stop=k == NHC - 1)
                        ins.then_inc(s["down_done"], 1)

                    def post(part):
                        if part == 0:
                            pe.wait_ge(s["wide_ready"], 1)
                            pe.wait_ge(s["weights_ready"], NS)
                            turn_all(lambda t: rdenom_wide[:, t * NH:(t + 1) * NH, :].rearrange("p h d -> p (h d)"),
                                     turn, "rdenom_turned")
                            return
                        for i in range(2):
                            half = slice(i * HALF, (i + 1) * HALF)
                            if part == 1:
                                pe.wait_ge(s["mix_ready"], i + 1)
                                nc.tensor.matmul(mixed[i][0:C // 4, :], se1_w[:], xnT[:, half],
                                                 start=True, stop=True).then_inc(s["se1_done"], 1)
                            elif part == 2:
                                pe.wait_ge(s["se1_ready"], i + 1)
                                nc.tensor.matmul(turn[i][:], se2_w[:], se_lin[:, half],
                                                 start=True, stop=True).then_inc(s["se2_done"], 1)
                            else:
                                pe.wait_ge(s["gated"], i + 1)
                                for t in range(4):
                                    col = i * HALF + t * P
                                    ins = nc.tensor.matmul(turn[i][:, t * C:(t + 1) * C], xnT[:, col:col + P],
                                                           out_w[:], start=True, stop=True)
                                ins.then_inc(s["out_done"], 1)

                    for what, n in plan:
                        if what == "ffn head" and n == 0:
                            ffn_turn()
                        elif what == "ffn head" and n == 1:
                            ffn_logits()
                        elif what == "ahead":
                            prepare(n)
                        elif what == "exponent":
                            exponent(n)
                        elif what == "product":
                            product(n)
                        elif what == "up":
                            unit_up(n)
                        elif what == "down":
                            unit_down(n)
                        elif what == "post":
                            post(n)

                @block.vector
                def _(dve):
                    seq = Chain(dve, s["dve_seq"])
                    V = nc.vector

                    def step_of(ins):
                        seq(ins)
                        seq.wait()

                    def over(a, n):
                        return a.unsqueeze(2).broadcast_to([P, a.shape[1], n])

                    def norm(a, src, var_done):
                        for t in range(NT):
                            ins = V.bn_stats(stats[:, a, t, :], src[:, t, :])
                        step_of(ins)
                        for t in range(NT):
                            ins = V.bn_aggr(mean_var[:, a, t, :], stats[:, a, t, :])
                        step_of(ins)
                        V.tensor_scalar(var_eps[:, a], mean_var[:, a, :, 1], EPS, None, ALU.add
                                        ).then_inc(s[var_done], 1)

                    def normalize(a, src, dst, rstd_done, done):
                        dve.wait_ge(s[rstd_done], 1)
                        for t in range(NT):
                            ins = V.tensor_scalar(dst[:, t, :], src[:, t, :], mean_var[:, a, t, 0:1],
                                                  rstd[:, a, t:t + 1], ALU.subtract, ALU.mult)
                        ins.then_inc(s[done], 1)

                    def choose():
                        dve.wait_ge(s["logits_done"], 1)
                        V.tensor_copy(logits[:].rearrange("p t e -> p (t e)"), down[:, 0:NT * NE]
                                      ).then_inc(s["logits_read"], 1)
                        dve.wait_ge(s["logits_read"], 1)
                        for t in range(NT):
                            ins = V.max(out=top[:, t, :], in_=logits[:, t, :])
                        step_of(ins)
                        V.tensor_tensor(gap[:], top[:, :, 1], top[:, :, 0], ALU.subtract
                                        ).then_inc(s["gap_ready"], 1)
                        for t in range(NT):
                            ins = V.max_index(out=top_id[:, t, :], in_max=top[:, t, :], in_values=logits[:, t, :])
                        step_of(ins)
                        V.tensor_copy(top_idf[:], top_id[:])

                    def gate_table():
                        dve.wait_ge(s["gap_tanh"], 1)
                        V.tensor_scalar(gate12[:, 0], gap[:], -0.5, 0.5, ALU.mult, ALU.add)
                        step_of(V.tensor_scalar(gate12[:, 1], gap[:], 0.5, 0.5, ALU.mult, ALU.add))
                        for i, dst in enumerate((gates, picked)):
                            step_of(V.tensor_tensor(dst[:], expert_ids[:].unsqueeze(1).broadcast_to([P, NT, NE]),
                                                    over(top_idf[:, :, i], NE), ALU.is_equal))
                            step_of(V.tensor_tensor(dst[:], dst[:], over(gate12[:, i], NE), ALU.mult))
                        seq(V.tensor_tensor(gates[:], gates[:], picked[:], ALU.add))

                    def ffn_low():
                        for i in range(2):
                            half = slice(i * HALF, (i + 1) * HALF)
                            dve.wait_ge(s["hi_ready"], i + 1)
                            dve.wait_ge(s["xn2T_ready"], i + 1)
                            V.tensor_tensor(xT_lo[:, half], xn2T[:, half], xT_hi[:, half].bitcast(F32),
                                            ALU.subtract).then_inc(s["lo_ready"], 1)

                    def prepare(part):
                        if part == 0:
                            if attention:
                                dve.wait_ge(s["x_loaded"], 16)
                            norm(0, x_in, "var_ready")
                        elif part == 1:
                            normalize(0, x_in, x_in, "rstd_ready", "x_ready")
                        elif part in (4, 5, 6):
                            g = part - 4
                            nt = min(3, NT - 3 * g)
                            dve.wait_ge(s["proj_done"], g + 1)
                            if ffn and g == 0:
                                dve.wait_ge(s["logits_done"], 1)
                                dve.wait_ge(s["lo_ready"], 2)
                            V.tensor_tensor(proj[:, 3 * g:3 * g + nt, :],
                                            ahead_ps[:, 0:nt * NP].rearrange("p (t n) -> p t n", n=NP),
                                            bias_proj[:].unsqueeze(1).broadcast_to([P, nt, NP]), ALU.add
                                            ).then_inc(s["proj_ready"], 1)
                        elif part == 7:
                            silus()
                        elif part == 8:
                            geometry()
                        elif part == 9:
                            parameters()
                        elif part == 10:
                            parameters_twice()
                        elif part == 11:
                            for j in range(2):
                                base(j, first=True)
                                slopes(j, first=True)

                    def silus():
                        dve.wait_ge(s["tanh_ready"], 1)
                        step_of(V.tensor_scalar(half_tanh, half_tanh, 0.5, 0.5, ALU.mult, ALU.add))
                        V.tensor_tensor(proj, proj, half_tanh, ALU.mult).then_inc(s["silu_ready"], 1)
                        dve.wait_ge(s["silu_ready"], 1)
                        qw = half_tanh[:, :, 0:NQ]
                        step_of(V.tensor_tensor(qw, proj[:, :, NW:NP],
                                                key_w[:].rearrange("p h d -> p (h d)").unsqueeze(1).broadcast_to([P, NT, NQ]),
                                                ALU.mult))
                        seq(V.tensor_reduce(qk[:], qw.rearrange("p t (h d) -> p t h d", d=D), AX, ALU.add))

                    def geometry():
                        dve.wait_ge(s["wave_ready"], 1)
                        step_of(V.tensor_reduce(wave_sum[:], wave[:], AX, ALU.add))
                        V.tensor_scalar(freq, wave_sum[:, :, 0], 7.5 / NH, 8.5, ALU.mult, ALU.add)
                        V.tensor_scalar(phase, wave_sum[:, :, 1], 16.0 / NH, None, ALU.mult)
                        step_of(V.tensor_scalar(decay[:], wave_sum[:, :, 2], 4.75 / NH, 5.25, ALU.mult, ALU.add))
                        V.reciprocal(rfreq, freq)
                        V.tensor_tensor(shift[:], centers, phase, ALU.add)
                        step_of(V.tensor_scalar(decay[:], decay[:], 0.1, None, ALU.max))
                        V.reciprocal(rdecay[:], decay[:])
                        step_of(V.tensor_scalar(shift[:], shift[:], -1.0, 0.5, ALU.mult, ALU.add))
                        V.tensor_tensor(shift2, shift[:], rfreq, ALU.mult).then_inc(s["geometry"], 1)
                        dve.wait_ge(s["geometry"], 1)

                    def parameters():
                        V.tensor_tensor(freq_decay[:], freq, rdecay[:], ALU.mult)
                        V.scalar_tensor_tensor(slope_s[:], qk[:], D ** -0.5, over(freq, NH), ALU.mult, ALU.mult)
                        step_of(V.tensor_tensor(pos[:], over(freq, 2 * MAXK + 1),
                                                strides[:].unsqueeze(1).broadcast_to([P, NT, 2 * MAXK + 1]), ALU.mult))
                        V.tensor_tensor(slope_e, slope_s[:], over(freq_decay[:], NH), ALU.subtract)
                        dve.wait_ge(s["geometry_twice"], 1)
                        V.tensor_copy(twice[:, :, 0:NG], ahead_ps[:, 0:2 * NG].rearrange("p (a n) -> p a n", a=2)
                                      ).then_inc(s["geometry_out"], 1)
                        step_of(V.tensor_tensor(pos[:], pos[:], over(centers, 2 * MAXK + 1), ALU.add))
                        step_of(V.tensor_tensor(pos[:], pos[:], over(phase, 2 * MAXK + 1), ALU.add))
                        step_of(V.tensor_scalar(valid[:], pos[:], 0.0, None, ALU.is_ge))
                        step_of(V.scalar_tensor_tensor(valid[:].rearrange("p t k -> p (t k)"),
                                                       pos[:].rearrange("p t k -> p (t k)"), float(L),
                                                       valid[:].rearrange("p t k -> p (t k)"),
                                                       ALU.is_lt, ALU.mult))
                        V.tensor_copy(some[:, :, 0:1], valid[:, :, 0:1])
                        step_of(V.tensor_tensor(some[:, :, 1:NK], valid[:, :, 1:NK], valid[:, :, NK:], ALU.add))
                        step_of(V.tensor_scalar(valid[:, :, 0:NK], some[:], 0.0, None, ALU.is_gt))
                        V.tensor_tensor(some2[:], valid[:, :, 0:NK],
                                        strides[:, 0:NK].unsqueeze(1).broadcast_to([P, NT, NK]), ALU.mult)
                        step_of(V.tensor_tensor(valid[:, :, 0:NK], valid[:, :, 0:NK],
                                                falling[:].unsqueeze(1).broadcast_to([P, NT, NK]), ALU.mult))
                        V.tensor_reduce(kmax, some2[:], AX, ALU.max)
                        step_of(V.tensor_reduce(kmin, valid[:, :, 0:NK], AX, ALU.max))
                        step_of(V.tensor_scalar(kmin, kmin, -1.0, float(MAXK), ALU.mult, ALU.add))
                        step_of(V.tensor_tensor(kept[:], strides[:, 0:NK].unsqueeze(1).broadcast_to([P, NT, NK]),
                                                over(kmin, NK), ALU.max))
                        V.tensor_tensor(kept[:], kept[:], over(kmax, NK), ALU.min)
                        V.tensor_tensor(end1[:], slope_s[:], over(kmax, NH), ALU.mult)
                        step_of(V.tensor_tensor(end2[:], slope_s[:], over(kmin, NH), ALU.mult))
                        step_of(V.tensor_tensor(end1[:], end1[:], end2[:], ALU.max))
                        V.tensor_scalar(neg_max[:], end1[:], -1.0, None, ALU.mult).then_inc(s["params"], 1)
                        dve.wait_ge(s["params"], 1)

                    def parameters_twice():
                        if attention:
                            for done in max_rows:
                                dve.wait_ge(done, 16 * (NT - 2))
                        dve.wait_ge(s["params_twice"], 1)
                        late = ahead_ps[:, 2 * NG:2 * NG + 2 * NR].rearrange("p (a n) -> p a n", a=2)
                        V.tensor_copy(twice[:, :, NG:], late[:, :, 0:2 * NT])
                        seq(V.tensor_copy(slope_parts[:], late[:, :, 2 * NT:]))
                        step_of(V.tensor_copy(max_parts[:, 0, :], ahead_ps[0:NT * NH, MAX_AT:MAX_AT + P]))
                        V.tensor_tensor(max_parts[:, 1, :], ahead_ps[0:NT * NH, MAX_AT:MAX_AT + P],
                                        max_parts[:, 0, :].bitcast(F32), ALU.subtract).then_inc(s["max_ready"], 1)
                        seq.wait()
                        low = slope_parts[HB:P]
                        step_of(V.tensor_tensor(low, late[HB:P, :, 2 * NT:], low.bitcast(F32), ALU.subtract))

                    def base(j, first=False):
                        _, _, lo, chunks = window(j)
                        w = chunks * P
                        k = j % 2
                        of = twice[:, k].rearrange("p (i t) -> p i t", t=NT)[:, :, j // 2:j // 2 + 1]
                        if first:
                            dve.wait_ge(s["first_candidates"], j + 1)
                            seq.wait()
                        else:
                            dve.wait_ge(s["candidates"], j - 1)
                        wait_exponents(j, first)
                        p, d = place[0:HB, k, 0:w], dist[:, k, 0:w]
                        bits = samp[:, k, 0:w].bitcast(U32)
                        seq(V.tensor_scalar(bits, bits, 0x7FFFFFFF, None, ALU.bitwise_and))
                        step_of(V.scalar_tensor_tensor(p, p, of[0:HB, 1], rows[0:HB, lo:lo + w],
                                                       ALU.add, ALU.subtract))
                        V.tensor_scalar(d, samp[:, k, 0:w], of[:, 5], of[:, 6], ALU.min, ALU.max)
                        step_of(V.tensor_scalar(above[:, 0:w], p, 1.0, None, ALU.is_ge))
                        V.scalar_tensor_tensor(miss[0:HB, k, 0:w], p, 0.0, above[:, 0:w], ALU.is_lt, ALU.add
                                               ).then_inc(s["first_windows" if first else "window_ready"], 1)

                    def wait_exponents(j, first):
                        if not first:
                            dve.wait_ge(s["exponents"], SLOTS_BEFORE[j - 1])
                        elif attention:
                            dve.wait_ge(s["exponents"], SLOTS_BEFORE[NJ - 1 + j])

                    def slopes(j, first=False):
                        wait_exponents(j, first)
                        part = slope_parts[:, j % 2, j // 2 * NH:(j // 2 + 1) * NH].bitcast(F32)
                        V.tensor_tensor(slope_diag[:, j % 2], half_ident[:].unsqueeze(1).broadcast_to([P, NH, HB]),
                                        over(part, HB), ALU.mult
                                        ).then_inc(s["first_windows" if first else "slopes_ready"], 1)

                    def denominators():
                        dve.wait_ge(s["sums_masked"], 2)
                        step_of(V.tensor_reduce(sum_zu[:], sums[:], AX, ALU.add))
                        step_of(V.scalar_tensor_tensor(denom[:], sum_zu[:, 0], 1e-8, sum_zu[:, 1], ALU.mult, ALU.add))
                        step_of(V.reciprocal(rdenom[:], denom[:]))
                        V.tensor_copy(rdenom_wide, over(rdenom[:], D)).then_inc(s["wide_ready"], 1)

                    def gather(t):
                        dve.wait_ge(s["mixed_slot"], SLOTS_BEFORE[2 * t + 2])
                        part = mixed[t % 2][:, 0:2 * P].rearrange("p (j q l) -> p q j l", j=2, q=2)
                        dst = xnT[:, t * P:(t + 1) * P].rearrange("p (j l) -> p j l", j=2)
                        step_of(V.tensor_scalar(dst, part[:, 0], parity[:, 0:1], None, ALU.mult))
                        V.scalar_tensor_tensor(dst, part[:, 1], parity[:, 1:2], dst, ALU.mult, ALU.add
                                               ).then_inc(s["gathered"], 1)

                    def unit(m):
                        hf, e = expert_of(m)
                        dve.wait_ge(s["down_done"], m + 1)
                        if m == 1:
                            seq.wait()
                        if m % (NE + 1):
                            dve.wait_ge(s["acc_done"], m)
                        t0 = hf * NT // 2
                        if e == NE:
                            V.tensor_tensor(acc[:, t0:t0 + NT // 2, :].rearrange("p t c -> p (t c)"), down[:],
                                            x1[:, t0:t0 + NT // 2, :].rearrange("p t c -> p (t c)"), ALU.add
                                            ).then_inc(s["acc_done"], 1)
                            return
                        for t in range(NT // 2):
                            a = acc[:, t0 + t, :]
                            ins = V.scalar_tensor_tensor(a, down[:, t * C:(t + 1) * C],
                                                         gates[:, t0 + t, e:e + 1], a, ALU.mult, ALU.add)
                        ins.then_inc(s["acc_done"], 1)

                    def post(part):
                        if part == 0:
                            dve.wait_ge(s["gathered"], NT)
                            for i in range(2):
                                half = slice(i * HALF, (i + 1) * HALF)
                                dve.wait_ge(s["rdenom_turned"], i + 1)
                                V.tensor_tensor(xnT[:, half], xnT[:, half], turn[i][:], ALU.mult
                                                ).then_inc(s["mix_ready"], 1)
                            return
                        for i in range(2):
                            half = slice(i * HALF, (i + 1) * HALF)
                            if part == 1:
                                dve.wait_ge(s["se1_tanh"], i + 1)
                                step_of(V.tensor_scalar(se_lin[:, half], mixed[i][0:C // 4, :],
                                                        se1_b[:, 0:1], 0.5, ALU.add, ALU.mult))
                                V.scalar_tensor_tensor(se_lin[:, half], se_tanh[:, half], 1.0, se_lin[:, half],
                                                       ALU.add, ALU.mult).then_inc(s["se1_ready"], 1)
                            elif part == 2:
                                dve.wait_ge(s["se2_tanh"], i + 1)
                                V.scalar_tensor_tensor(xnT[:, half], se_gate[:, half], 1.0, xnT[:, half],
                                                       ALU.add, ALU.mult).then_inc(s["gated"], 1)
                            else:
                                if i == 0:
                                    dve.wait_ge(s["res_loaded"], 16)
                                dve.wait_ge(s["out_tanh_ready"], i + 1)
                                step_of(V.scalar_tensor_tensor(attn[:, half], out_tanh[:, half], 1.0, turn[i][:],
                                                               ALU.add, ALU.mult))
                                V.scalar_tensor_tensor(x1[:, 4 * i:4 * i + 4, :].rearrange("p t c -> p (t c)"),
                                                       attn[:, half], 0.5,
                                                       x_res[:, 4 * i:4 * i + 4, :].rearrange("p t c -> p (t c)"),
                                                       ALU.mult, ALU.add)

                    for what, n in plan:
                        if what == "ffn norm" and n == 0:
                            norm(1, x1, "var2_ready")
                        elif what == "ffn norm":
                            normalize(1, x1, xn2, "rstd2_ready", "xn2_ready")
                        elif what == "ffn head" and n == 0:
                            ffn_low()
                        elif what == "ffn head" and n == 1:
                            choose()
                        elif what == "ffn head" and n == 3:
                            gate_table()
                        elif what == "ahead":
                            prepare(n)
                        elif what == "base":
                            base(n)
                        elif what == "sums" and n == 7:
                            denominators()
                        elif what == "slopes":
                            slopes(n)
                        elif what == "gather":
                            gather(n)
                        elif what == "down":
                            unit(n)
                        elif what == "post":
                            post(n)
            clear_semaphores()

        setup()
        clear_semaphores()
        step(-1, False, False, True)
        step(0, True, False, True)
        with nc.Fori(1, B) as b:
            step(b, True, True, True)
        step(B, False, True, False)


_INS = ['L0_attn_x', 'L0_attn_w_wave', 'L0_attn_b_wave', 'L0_attn_w_query', 'L0_attn_b_query',
        'L0_attn_key_weight', 'L0_attn_w_se1', 'L0_attn_b_se1', 'L0_attn_w_se2', 'L0_attn_b_se2',
        'L0_attn_w_out', 'L0_ffn_shared_w1', 'L0_ffn_shared_w2', 'L0_ffn_experts_w1',
        'L0_ffn_experts_w2', 'L0_ffn_gate_w']


def kernel(**inputs):
    import numpy as np
    import concourse.bacc as bacc
    from concourse.bass_utils import run_bass_kernel_spmd

    nc = bacc.Bacc("TRN2", target_bir_lowering=False, num_devices=1)
    arrays, args = {}, []
    for name in _INS:
        a = np.ascontiguousarray(inputs[name])
        arrays[f"in_{name}"] = a
        args.append(nc.dram_tensor(f"in_{name}", a.shape, mybir.dt.from_np(a.dtype), kind="ExternalInput").ap())
    shape = inputs['L0_attn_x'].shape
    result = nc.dram_tensor("out_x", shape, mybir.dt.float32, kind="ExternalOutput").ap()
    build_program(nc, *args, result)
    r = run_bass_kernel_spmd(nc, [arrays], core_ids=[0])
    return r.results[0]["out_x"]
```

```python
from contextlib import ExitStack

import concourse.bass as bass
from concourse import mybir


def build_program(nc, x, w_wave, b_wave, w_query, b_query, key_weight, w_se1, b_se1, w_se2, b_se2,
                  w_out, shared_w1, shared_w2, experts_w1, experts_w2, gate_w, out):
    F32, F32R = mybir.dt.float32, mybir.dt.float32r
    U32 = mybir.dt.uint32
    ALU = mybir.AluOpType
    ACT = mybir.ActivationFunctionType
    AX = mybir.AxisListType.X

    P = 128
    B, L, C = x.shape
    NT = L // P
    NH = w_wave.shape[1] // 3
    D = C // NH
    NW, NQ = w_wave.shape[1], w_query.shape[1]
    NP = NW + NQ
    MAXK = 16
    NK = MAXK + 1
    NE = experts_w1.shape[0]
    HID = experts_w1.shape[1]
    NHC = HID // P
    HALF = L // 2
    EPS = 1e-5
    LOW, HIGH = 264, 336
    MAGIC = float(3 * 2 ** 22)
    NU = 2 * (NE + 1)

    HB = P // 2
    NJ = L // HB

    def window(j):
        first, end = j * HB - LOW, j * HB + HIGH
        if first < 0:
            return 0, 0, 0, -(-end // P)
        if end > L:
            c = first // P
            return 0, c, c * P, NT - c
        copy = 1 if first % P == SHIFTS[1] else 2
        return copy, first // P, first, -(-(end - first) // P)

    SHIFTS = (0, (-LOW) % P, (HB - LOW) % P)
    SLOTS = [(j, i) for j in range(NJ) for i in range(window(j)[3])]
    SLOTS_BEFORE = [sum(window(k)[3] for k in range(j)) for j in range(NJ + 1)]
    NS = len(SLOTS)
    WMAX = P * max(window(j)[3] for j in range(NJ))
    MISS = -256.0
    UNITS_AFTER = (2, 2, 2, 2, 2, 2, 2, 1)
    BEHIND = {
        0: [("ffn norm", 1)],
        1: [("ffn head", 0), ("ffn head", 1)],
        2: [("ffn head", 2), ("ffn head", 3)],
        3: [("ahead", 0)],
        4: [("sums", 0), ("ahead root", 0)],
        5: [("sums", 1), ("ahead", 1)],
        6: [("sums", 2), ("ahead", 2)],
        7: [("sums", 3), ("ahead", 3)],
        8: [("sums", 4), ("ahead", 4)],
        9: [("sums", 5), ("ahead", 5)],
        10: [("sums", 6), ("ahead", 6)],
        11: [("sums", 7)],
        12: [("ahead", 7)],
        13: [("ahead", 8)],
        14: [("ahead", 9)],
    }
    TAIL = [("post", 0), "unit", ("post", 1), ("ahead", 10), "unit", ("post", 2), ("ahead", 11), "unit",
            ("ahead", 12), ("post", 3), "unit", ("post", 4), "unit"]
    NX, NWT = 3, 4
    LAG = 3

    ctx = ExitStack()
    with ctx:
        def sb(name, shape, dt=F32):
            return ctx.enter_context(nc.sbuf_tensor(name, shape, dt))

        def sem(name):
            return ctx.enter_context(nc.semaphore(name))

        ident = sb("ident", [P, P])
        rows = sb("rows", [P, L])
        half_ident = sb("half_ident", [P, HB])
        pick = sb("pick", [P, 2, P])
        parity = sb("parity", [P, 2])
        strides = sb("strides", [P, 2 * MAXK + 1])
        falling = sb("falling", [P, NK])
        minus_half = sb("minus_half", [P, 2, NT])
        expert_ids = sb("expert_ids", [P, NE])
        w_proj = sb("w_proj", [P, NP])
        bias_proj = sb("bias_proj", [P, NP])
        key_w = sb("key_w", [P, NH, D])
        se1_w = sb("se1_w", [P, C // 4])
        se2_w = sb("se2_w", [C // 4, C])
        se1_b = sb("se1_b", [C // 4, 2])
        se2_b = sb("se2_b", [C, 2])
        out_w = sb("out_w", [P, C])
        gate_raw = sb("gate_raw", [NE, C])
        gate_wT = sb("gate_wT", [P, NE])
        w1_hi = sb("w1_hi", [P, NE + 1, HID], F32R)
        w1_lo = sb("w1_lo", [P, NE + 1, HID], F32R)
        w2T = sb("w2T", [P, NE + 1, NHC, C])

        x_in = sb("x_in", [P, NT, C])
        x_res = sb("x_res", [P, NT, C])
        xn = sb("xn", [P, NT, C])
        xnT = sb("xnT", [P, L])
        stats = sb("stats", [P, 2, NT, 6])
        mean_var = sb("mean_var", [P, 2, NT, 2])
        var_eps = sb("var_eps", [P, 2, NT])
        rstd = sb("rstd", [P, 2, NT])
        wave = sb("wave", [P, NT, 3, NH])
        wave_sum = sb("wave_sum", [P, NT, 3])
        decay = sb("decay", [P, NT])
        rdecay = sb("rdecay", [P, NT])
        freq_decay = sb("freq_decay", [P, NT])
        shift = sb("shift", [P, NT])
        qk = sb("qk", [P, NT, NH])
        slope_s = sb("slope_s", [P, NT, NH])
        token = sb("token", [P, 7 * NT + NT * NH])
        freq, phase, centers, rfreq, shift2, kmax, kmin = (token[:, i * NT:(i + 1) * NT] for i in range(7))
        slope_e = token[:, 7 * NT:].rearrange("p (t h) -> p t h", h=NH)
        twice = sb("twice", [P, 2, 7 * NT])
        slope_parts = sb("slope_parts", [P, 2, NT * NH], F32R)
        max_parts = sb("max_parts", [NT * NH, 2, P], F32R)
        end1 = sb("end1", [P, NT, NH])
        end2 = sb("end2", [P, NT, NH])
        neg_max = sb("neg_max", [P, NT, NH])
        pos = sb("pos", [P, NT, 2 * MAXK + 1])
        valid = sb("valid", [P, NT, 2 * MAXK + 1])
        some = sb("some", [P, NT, NK])
        some2 = sb("some2", [P, NT, NK])
        kept = some2
        sums = sb("sums", [P, 2, NT * NH, NK])
        half_tanh = sums[:].rearrange("p a n k -> p (a n k)")[:, 0:NT * NP].rearrange("p (t n) -> p t n", t=NT)
        sum_zu = sb("sum_zu", [P, 2, NT * NH])
        denom = sb("denom", [P, NT * NH])
        rdenom = sb("rdenom", [P, NT * NH])

        samp = sb("samp", [P, 2, WMAX])
        place = sb("place", [HB, 2, WMAX])
        above = sb("above", [HB, WMAX])
        dist = sb("dist", [P, 2, WMAX], F32R)
        miss = sb("miss", [HB + 2, 2, WMAX], F32R)
        slope_diag = sb("slope_diag", [P, 2, NH, HB], F32R)
        miss_diag = sb("miss_diag", [HB + 2, 2, NH, P], F32R)
        weightT = sb("weightT", [P, NWT, NH * HB])

        x1 = sb("x1", [P, NT, C])
        acc = sb("acc", [P, NT, C])
        xT_hi = sb("xT_hi", [P, L], F32R)
        xT_lo = sb("xT_lo", [P, L], F32R)
        hidden = sb("hidden", [P, 2, NHC, HALF])
        gates = sb("gates", [P, NT, NE])
        logits = sb("logits", [P, NT, NE])
        top = sb("top", [P, NT, 8])
        top_id = sb("top_id", [P, NT, 8], U32)
        top_idf = end2
        gap = sb("gap", [P, NT])
        gate12 = sb("gate12", [P, 2, NT])
        picked = logits

        raw = hidden[:].rearrange("p a k n -> p (a k) n")
        shared = sb("shared", [P, 8 * L])
        moved = shared[:, 0:2 * (NT - 1) * C].rearrange("p (a t c) -> p a t c", a=2, c=C)
        proj = shared[:, 5 * L:5 * L + NT * NP].rearrange("p (t n) -> p t n", t=NT)
        se_tanh, se_lin = shared[0:C // 4, 0:L], shared[0:C // 4, L:2 * L]
        se_gate, out_tanh, attn = shared[:, 2 * L:3 * L], shared[:, 3 * L:4 * L], shared[:, 4 * L:5 * L]
        xn2 = shared[:, 5 * L:6 * L].rearrange("p (t c) -> p t c", t=NT)
        xn2T = shared[:, 6 * L:7 * L]
        next_xT = shared[:, 7 * L:8 * L]
        rdenom_wide = shared[:, 4 * L:5 * L].rearrange("p (n d) -> p n d", d=D)

        bank = [ctx.enter_context(nc.psum_tensor(f"bank{i}", [P, 512], F32)) for i in range(8)]
        turn = bank[0:NX]
        ahead_ps = bank[3]
        mixed = bank[4]
        gate_ps = (mixed, turn[2])
        up = bank[5:7]
        down = bank[7]
        NTU = NT // 2
        NGW = 2 * (NE + 1)
        NG = 5 * NT
        NR = 2 * NT + NT * NH
        MAX_AT = 2 * NG + 2 * NR

        names = ("setup_consts raw_loaded_even raw_loaded_odd small_loaded gate_turned weights_turned "
                 "weights_hi weights_free x_loaded res_loaded var2_ready rstd2_ready var_ready "
                 "rstd_ready x_ready rows_moved xn_turned xnT_ready proj_done proj_ready tanh_ready "
                 "silu_ready wave_ready geometry geometry_twice geometry_out params params_twice "
                 "max_ready max_rows_even max_rows_odd sums_ready sums_exp sums_masked wide_ready "
                 "candidates window_ready slopes_ready parts_ready first_slopes first_candidates "
                 "first_windows first_rows exponents weights_ready mixed_slot gathered rdenom_turned "
                 "mix_ready se1_done se1_tanh se1_ready se2_done se2_tanh gated out_done out_tanh_ready "
                 "xn2_ready xn2_turned xn2T_ready hi_ready lo_ready logits_done logits_read gap_ready "
                 "gap_tanh up_done silu_done down_done acc_done stored dve_seq pool_seq").split()
        s = {n: sem(n) for n in names}
        raw_loaded = (s["raw_loaded_even"], s["raw_loaded_odd"])
        max_rows = (s["max_rows_even"], s["max_rows_odd"])

        x_dram = x.rearrange("b (t p) c -> p (b t) c", p=P)
        out_dram = out.rearrange("b (t p) c -> p (b t) c", p=P)

        class Chain:

            def __init__(self, eng, sem):
                self.eng, self.sem, self.n = eng, sem, 0

            def __call__(self, ins):
                self.n += 1
                ins.then_inc(self.sem, 1)

            def wait(self):
                self.eng.wait_ge(self.sem, self.n)

        def clear_semaphores():
            with nc.Block(no_gpsimd_drain=True) as block:
                @block.sync
                def _(sp):
                    for n in names[0::4]:
                        sp.sem_clear(s[n])

                @block.scalar
                def _(act):
                    for n in names[1::4]:
                        act.sem_clear(s[n])

                @block.vector
                def _(dve):
                    for n in names[2::4]:
                        dve.sem_clear(s[n])

                @block.tensor
                def _(pe):
                    for n in names[3::4]:
                        pe.sem_clear(s[n])

        def setup():
            with nc.Block() as block:
                @block.sync
                def _(sp):
                    sp.dma_start(x_in[:], x_dram[:, 0:NT, :]).then_inc(s["x_loaded"], 16)
                    sp.wait_ge(s["x_loaded"], 16)

                @block.gpsimd
                def _(pool):
                    seq = Chain(pool, s["pool_seq"])
                    seq(nc.gpsimd.memset(ident[:], 0.0))
                    seq.wait()
                    nc.gpsimd.affine_select(out=ident[:], in_=ident[:], compare_op=ALU.not_equal, fill=1.0,
                                            base=0, pattern=[[-1, P]], channel_multiplier=1)
                    nc.gpsimd.memset(minus_half[:], -0.5)
                    iota = dict(allow_small_or_imprecise_dtypes=True)
                    nc.gpsimd.iota(rows[:], [[1, L]], base=0, channel_multiplier=0, **iota)
                    nc.gpsimd.iota(centers, [[P, NT]], base=0, channel_multiplier=1, **iota)
                    nc.gpsimd.iota(strides[:, 0:NK], [[1, NK]], base=0, channel_multiplier=0, **iota)
                    nc.gpsimd.iota(strides[:, NK:], [[-1, MAXK]], base=-1, channel_multiplier=0, **iota)
                    nc.gpsimd.iota(falling[:], [[-1, NK]], base=MAXK, channel_multiplier=0, **iota)
                    nc.gpsimd.iota(expert_ids[:], [[1, NE]], base=0, channel_multiplier=0,
                                   **iota).then_inc(s["setup_consts"], 1)

                @block.scalar
                def _(act):
                    small = [(w_proj[:, 0:NW], w_wave), (w_proj[:, NW:NP], w_query),
                             (bias_proj[:, 0:NW], b_wave.partition_broadcast(P)),
                             (bias_proj[:, NW:NP], b_query.partition_broadcast(P)),
                             (key_w[:, 0, :], key_weight.partition_broadcast(P)),
                             (se1_w[:], w_se1), (se2_w[:], w_se2),
                             (se1_b[:, 0:1], b_se1.rearrange("(p a) -> p a", a=1)),
                             (se2_b[:, 0:1], b_se2.rearrange("(p a) -> p a", a=1)),
                             (out_w[:], w_out), (gate_raw[:], gate_w)]
                    for dst, src in small:
                        act.dma_start(dst, src).then_inc(s["small_loaded"], 16)
                    act.wait_ge(s["gate_turned"], 1)
                    nc.scalar.activation(gate_wT[:], mixed[:, 0:NE], ACT.Copy)

                @block.tensor
                def _(pe):
                    pe.wait_ge(s["setup_consts"], 1)
                    pe.wait_ge(s["small_loaded"], 16 * 11)
                    nc.tensor.transpose(mixed[:, 0:NE], gate_raw[:], ident[0:NE, 0:NE]
                                        ).then_inc(s["gate_turned"], 1)

                @block.vector
                def _(dve):
                    dve.wait_ge(s["setup_consts"], 1)
                    for hf in range(2):
                        for i in range(2):
                            nc.vector.tensor_copy(pick[:, hf, i * HB:(i + 1) * HB], ident[:, hf * HB:(hf + 1) * HB])
                    nc.vector.tensor_tensor(half_ident[:], ident[:, 0:HB], ident[:, HB:P], ALU.add)
                    nc.vector.tensor_reduce(stats[:, 0, 0:2, 0:4], ident[:].rearrange(
                        "p (g q d) -> p q g d", q=2, d=D), AX, ALU.add).then_inc(s["dve_seq"], 1)
                    dve.wait_ge(s["dve_seq"], 1)
                    nc.vector.tensor_reduce(parity[:], stats[:, 0, 0:2, 0:4], AX, ALU.add)
                    for r in range(2):
                        for h in range(NH):
                            for i in range(2):
                                nc.vector.tensor_scalar(miss_diag[0:HB, r, h, i * HB:(i + 1) * HB],
                                                        ident[0:HB, 0:HB], MISS, None, ALU.mult)
                    for k in range(2):
                        nc.vector.tensor_scalar(miss[HB:HB + 2, k, :], rows[HB:HB + 2, 0:WMAX], 0.0, 1.0,
                                                ALU.mult, ALU.add)
                    dve.wait_ge(s["small_loaded"], 16 * 11)
                    for h in range(1, NH):
                        nc.vector.tensor_copy(key_w[:, h, :], key_w[:, 0, :])
                    nc.vector.tensor_scalar(se1_b[:, 1:2], se1_b[:, 0:1], 0.5, None, ALU.mult)
                    nc.vector.tensor_scalar(se2_b[:, 1:2], se2_b[:, 0:1], 0.5, None, ALU.mult)
                    nc.vector.tensor_scalar(out_w[:], out_w[:], 0.5, None, ALU.mult)

        def step(b, attention, ffn, ahead):
            plan = []
            units = []
            for m in range(NU + 1) if ffn else ():
                ups = [("up", m * NHC + k) for k in range(NHC)] if m < NU else []
                downs = [("down part", (m - 1) * NTU + k) for k in range(NTU)] + [("down", m - 1)] if m else []
                units.append((ups, downs))

            def next_unit():
                return units.pop(0) if units else ([], [])

            def ffn_units(n):
                for _ in range(n):
                    ups, downs = next_unit()
                    plan.extend(ups[0:2] + downs + ups[2:])

            def begin(n):
                plan.extend([("exponent", n), ("exp", n)])

            behind = {j: [] for j in range(NJ)}
            for j in range(NJ - 2):
                behind[j] += [("base", j + 2), ("slopes", j + 2)]
            for j, items in BEHIND.items():
                behind[j] += items
            if not ffn:
                for g in range(NGW):
                    behind[2 + g // 2].append(("weights", g))

            plan.append(("ffn norm", 0))
            if attention:
                begun = 0
                for t in range(NT):
                    for n in range(SLOTS_BEFORE[2 * t], SLOTS_BEFORE[2 * t + 2]):
                        if n >= begun:
                            begin(n)
                            begun = n + 1
                        if n - LAG >= SLOTS_BEFORE[2 * t]:
                            plan.append(("product", n - LAG))
                        j, i = SLOTS[n]
                        if i == window(j)[3] - 1:
                            plan += behind[j]
                            if j + 2 < NJ and j % 2 == 0:
                                plan.append(("window", j + 2))
                    last = SLOTS_BEFORE[2 * t + 2] - 1
                    ups, downs = next_unit() if UNITS_AFTER[t] else ([], [])
                    plan += ups[0:1] + [("product", last - 2), ("product", last - 1)] + ups[1:2] + [("product", last)]
                    plan += [("gather", t)] + [("window", 2 * t + 3)] * (2 * t + 3 < NJ)
                    plan += downs + ups[2:]
                    ups, downs = [], []
                    if UNITS_AFTER[t] > 1:
                        ffn_units(UNITS_AFTER[t] - 2)
                        ups, downs = next_unit()
                    plan += ups
                    if t + 1 < NT:
                        for n in range(last + 1, last + 3):
                            begin(n)
                            begun = n + 1
                    plan += downs
                for item in TAIL:
                    if item == "unit":
                        ffn_units(1)
                    else:
                        plan.append(item)
            else:
                plan += [("ffn norm", 1), ("ffn head", 0), ("ffn head", 1), ("ffn head", 2), ("ffn head", 3)]
                plan.append(("ahead root", 0))
                plan += [("ahead", k) for k in range(13)]
            ffn_units(len(units))
            if not ahead:
                plan = [item for item in plan if not item[0].startswith("ahead")]
            if not ffn:
                plan = [item for item in plan if not item[0].startswith("ffn")]
            if not attention:
                plan = [item for item in plan if item[0] != "sums"]

            def expert_of(m):
                return m // (NE + 1), (m - 1) % (NE + 1) if m % (NE + 1) else NE

            with nc.Block(no_gpsimd_drain=True) as block:

                @block.sync
                def _(sp):
                    def load_max_rows(t, done):
                        for part in range(2):
                            sp.dma_start(miss_diag[HB + part:HB + part + 1, t % 2].bitcast(F32),
                                         max_parts[t * NH:(t + 1) * NH, part, :].bitcast(F32)).then_inc(done, 16)

                    def store(hf):
                        sp.dma_start(out_dram[:, bass.ds((b - 1) * NT + hf * NT // 2, NT // 2), :],
                                     acc[:, hf * NT // 2:(hf + 1) * NT // 2]).then_inc(s["stored"], 16)

                    if attention:
                        sp.dma_start(x_res[:], x_dram[:, bass.ds(b * NT, NT), :]).then_inc(s["res_loaded"], 16)
                        for a in range(2):
                            r = SHIFTS[a + 1]
                            sp.dma_start(moved[0:P - r, a], xn[r:P, 0:NT - 1]).then_inc(s["rows_moved"], 16)
                            sp.dma_start(moved[P - r:P, a], xn[0:r, 1:NT]).then_inc(s["rows_moved"], 16)
                        if ahead:
                            sp.dma_start(x_in[:], x_dram[:, bass.ds((b + 1) % B * NT, NT), :]
                                         ).then_inc(s["x_loaded"], 16)
                        for t in range(2, NT):
                            sp.wait_ge(s["exponents"], SLOTS_BEFORE[2 * t - 2])
                            load_max_rows(t, max_rows[t % 2])
                    if ffn:
                        sp.wait_ge(s["acc_done"], NE + 1)
                        store(0)
                    if ahead:
                        sp.wait_ge(s["max_ready"], 1)
                        for t in range(2):
                            load_max_rows(t, s["first_rows"])
                    if ffn:
                        sp.wait_ge(s["acc_done"], 2 * (NE + 1))
                        store(1)
                        sp.wait_ge(s["stored"], 32)
                    if attention:
                        sp.wait_ge(max_rows[0], 16 * (NT - 2))
                        sp.wait_ge(max_rows[1], 16 * (NT - 2))
                        sp.wait_ge(s["rows_moved"], 64)
                        sp.wait_ge(s["res_loaded"], 16)
                    if ahead:
                        sp.wait_ge(s["first_rows"], 64)
                        if attention:
                            sp.wait_ge(s["x_loaded"], 16)

                @block.gpsimd
                def _(pool):
                    seq = Chain(pool, s["pool_seq"])

                    def reciprocal_root(a):
                        pool.wait_ge(s[("var_ready", "var2_ready")[a]], 1)
                        nc.gpsimd.tensor_tensor(rstd[:, a], var_eps[:, a], minus_half[:, a], ALU.pow
                                                ).then_inc(s[("rstd_ready", "rstd2_ready")[a]], 1)

                    def base(j, first=False):
                        _, _, lo, chunks = window(j)
                        w = chunks * P
                        k = j % 2
                        of = twice[:, k].rearrange("p (i t) -> p i t", t=NT)[:, :, j // 2:j // 2 + 1]
                        if first:
                            pool.wait_ge(s["geometry_out"], 1)
                            if attention:
                                pool.wait_ge(s["window_ready"], NJ - 2)
                        elif j >= 4:
                            pool.wait_ge(s["window_ready"], j - 3)
                        r = samp[:, k, 0:w]
                        seq(nc.gpsimd.tensor_scalar(r, rows[:, lo:lo + w], of[:, 3], of[:, 4], ALU.mult, ALU.add))
                        seq.wait()
                        nc.gpsimd.tensor_scalar(r, r, MAGIC, MAGIC - MAXK, ALU.add, ALU.max
                                                ).then_inc(s["first_candidates" if first else "candidates"], 1)

                    def slopes(j, first=False):
                        if first:
                            pool.wait_ge(s["parts_ready"], 1)
                        if not first:
                            pool.wait_ge(s["exponents"], SLOTS_BEFORE[j - 1])
                        elif attention:
                            pool.wait_ge(s["exponents"], SLOTS_BEFORE[NJ - 1 + j])
                        part = slope_parts[:, j % 2, j // 2 * NH:(j // 2 + 1) * NH].bitcast(F32)
                        nc.gpsimd.tensor_tensor(slope_diag[:, j % 2], half_ident[:].unsqueeze(1).broadcast_to([P, NH, HB]),
                                        part.unsqueeze(2).broadcast_to([P, NH, HB]), ALU.mult
                                        ).then_inc(s["first_slopes" if first else "slopes_ready"], 1)

                    def terms(part):
                        a = part % 2
                        v = sums[:, a].rearrange("p (t h) k -> p t h k", t=NT)
                        if part < 2:
                            seq(nc.gpsimd.tensor_tensor(
                                v, (slope_s[:], slope_e)[a].unsqueeze(3).broadcast_to([P, NT, NH, NK]),
                                kept[:].unsqueeze(2).broadcast_to([P, NT, NH, NK]), ALU.mult))
                        elif part < 4:
                            seq.wait()
                            nc.gpsimd.tensor_tensor(
                                v, v, neg_max[:].unsqueeze(3).broadcast_to([P, NT, NH, NK]), ALU.add
                                ).then_inc(s["sums_ready"], 1)
                        else:
                            pool.wait_ge(s["sums_exp"], 1)
                            nc.gpsimd.tensor_tensor(
                                v, v, some[:].unsqueeze(2).broadcast_to([P, NT, NH, NK]), ALU.mult
                                ).then_inc(s["sums_masked"], 1)

                    for what, n in plan:
                        if what == "ffn norm" and n == 0:
                            reciprocal_root(1)
                        elif what == "ahead root":
                            reciprocal_root(0)
                        elif what == "ahead" and n in (11, 12):
                            base(n - 11, first=True)
                            slopes(n - 11, first=True)
                            if n == 12:
                                pool.wait_ge(s["first_slopes"], 2)
                        elif what == "base":
                            base(n)
                        elif what == "slopes":
                            slopes(n)
                        elif what == "sums" and n != 4 and n != 7:
                            terms(n if n < 4 else n - 1)

                @block.scalar
                def _(act):
                    def copy(dst, src):
                        return nc.scalar.activation(dst, src, ACT.Copy)

                    def load_weights(batch):
                        for g in range(4 * batch, min(4 * batch + 4, NGW)):
                            e = g % (NE + 1)
                            w1, w2 = (experts_w1[e], experts_w2[e]) if e < NE else (shared_w1, shared_w2)
                            src = w1.rearrange("(k p) d -> p k d", p=P) if g <= NE else w2
                            dst = raw[:, g % 8, :]
                            if g <= NE:
                                dst = dst.rearrange("p (k d) -> p k d", d=C)
                            act.dma_start(dst, src).then_inc(raw_loaded[batch % 2], 16)

                    def keep_weights(g):
                        act.wait_ge(s["weights_turned"], g + 1)
                        e = g % (NE + 1)
                        dst = w1_hi[:, e, :] if g <= NE else w2T[:, e].rearrange("p k d -> p (k d)")
                        copy(dst, up[g % 2][:]).then_inc(s["weights_hi"], 1)
                        if g % 4 == 3:
                            load_weights(g // 4 + 2)

                    def ffn_head():
                        for i in range(2):
                            act.wait_ge(s["xn2_turned"], i + 1)
                            copy(xT_hi[:, i * HALF:(i + 1) * HALF], up[i][:]).then_inc(s["hi_ready"], 1)
                            copy(xn2T[:, i * HALF:(i + 1) * HALF], up[i][:]).then_inc(s["xn2T_ready"], 1)

                    def gap_tanh():
                        act.wait_ge(s["gap_ready"], 1)
                        nc.scalar.activation(gap[:], gap[:], ACT.Tanh, scale=0.5).then_inc(s["gap_tanh"], 1)

                    def prepare(part):
                        if part in (2, 3):
                            i = part - 2
                            act.wait_ge(s["xn_turned"], i + 1)
                            copy(next_xT[:, i * HALF:(i + 1) * HALF], ahead_ps[:]).then_inc(s["xnT_ready"], 1)
                        elif part == 7:
                            act.wait_ge(s["proj_ready"], 3)
                            if attention:
                                act.wait_ge(s["wide_ready"], 1)
                            nc.scalar.activation(half_tanh, proj, ACT.Tanh, scale=0.5
                                                 ).then_inc(s["tanh_ready"], 1)
                        elif part == 11:
                            if attention:
                                act.wait_ge(s["mixed_slot"], NS)
                            act.wait_ge(s["x_ready"], 1)
                            copy(xn[:], x_in[:])
                        elif part == 8:
                            act.wait_ge(s["silu_ready"], 1)
                            wv = proj[:, :, 0:NW].rearrange("p t (k h) -> p t k h", k=3)
                            nc.scalar.activation(wave[:, :, 0:3:2, :], wv[:, :, 0:3:2, :], ACT.Tanh, scale=0.5)
                            nc.scalar.activation(wave[:, :, 1, :], wv[:, :, 1, :], ACT.Tanh
                                                 ).then_inc(s["wave_ready"], 1)

                    def exps(n):
                        act.wait_ge(s["exponents"], n + 1)
                        if n >= NWT:
                            act.wait_ge(s["mixed_slot"], n - NWT + 1)
                        nc.scalar.activation(weightT[:, n % NWT], turn[n % NX][:], ACT.Exp
                                             ).then_inc(s["weights_ready"], 1)

                    def sums_exp():
                        act.wait_ge(s["sums_ready"], 2)
                        flat = sums[:].rearrange("p a n k -> p (a n k)")
                        nc.scalar.activation(flat, flat, ACT.Exp).then_inc(s["sums_exp"], 1)

                    def unit(n):
                        m, k = n // NHC, n % NHC
                        if m >= 2 and k == 0:
                            act.wait_ge(s["down_done"], m - 1)
                        act.wait_ge(s["up_done"], n + 1)
                        nc.scalar.activation(hidden[:, m % 2, k, :], up[n % 2][:], ACT.Silu
                                             ).then_inc(s["silu_done"], 1)

                    def post(part):
                        for i in range(2):
                            half = slice(i * HALF, (i + 1) * HALF)
                            if part == 1:
                                act.wait_ge(s["se1_done"], i + 1)
                                nc.scalar.activation(se_tanh[:, half], gate_ps[i][0:C // 4, :], ACT.Tanh,
                                                     scale=0.5, bias=se1_b[:, 1:2]).then_inc(s["se1_tanh"], 1)
                            elif part == 2:
                                act.wait_ge(s["se2_done"], i + 1)
                                nc.scalar.activation(se_gate[:, half], turn[i][:], ACT.Tanh,
                                                     scale=0.5, bias=se2_b[:, 1:2]).then_inc(s["se2_tanh"], 1)
                            elif part == 3 + i:
                                act.wait_ge(s["out_done"], i + 1)
                                nc.scalar.activation(out_tanh[:, half], turn[i][:], ACT.Tanh,
                                                     scale=0.5).then_inc(s["out_tanh_ready"], 1)

                    if attention and not ffn:
                        load_weights(0)
                        load_weights(1)
                    for what, n in plan:
                        if what == "weights":
                            keep_weights(n)
                        elif what == "ffn head" and n == 0:
                            ffn_head()
                        elif what == "ffn head" and n == 2:
                            gap_tanh()
                        elif what == "ahead":
                            prepare(n)
                        elif what == "exp":
                            exps(n)
                        elif what == "sums" and n == 4:
                            sums_exp()
                        elif what == "up":
                            unit(n)
                        elif what == "post":
                            post(n)

                @block.tensor
                def _(pe):
                    def turn_all(src, banks, signal):
                        for i, ps in enumerate(banks):
                            turn_four(lambda t: src(4 * i + t), ps, signal)

                    def turn_four(src, ps, signal):
                        for t in range(4):
                            ins = nc.tensor.transpose(ps[:, t * P:(t + 1) * P], src(t), ident[:])
                        ins.then_inc(s[signal], 1)

                    def turn_weights(g):
                        if g % 4 == 0:
                            pe.wait_ge(raw_loaded[g // 4 % 2], 16 * (4 * (g // 8) + min(4, NGW - g)))
                        if g >= 2:
                            pe.wait_ge(s["weights_hi"], g - 1)
                            pe.wait_ge(s["weights_free"], min(g - 1, NE + 1))
                        for k in range(NHC):
                            ins = nc.tensor.transpose(up[g % 2][:, k * P:(k + 1) * P],
                                                      raw[:, g % 8, k * P:(k + 1) * P], ident[:])
                        ins.then_inc(s["weights_turned"], 1)

                    def ffn_turn():
                        pe.wait_ge(s["xn2_ready"], 1)
                        turn_all(lambda t: xn2[:, t, :], up, "xn2_turned")

                    def ffn_logits():
                        pe.wait_ge(s["xn2T_ready"], 2)
                        for t in range(NT):
                            ins = nc.tensor.matmul(ahead_ps[:, t * NE:(t + 1) * NE], xn2T[:, t * P:(t + 1) * P],
                                                   gate_wT[:], start=True, stop=True)
                        ins.then_inc(s["logits_done"], 1)

                    def prepare(part):
                        if part in (2, 3):
                            i = part - 2
                            pe.wait_ge(s["x_ready"], 1)
                            if ffn and not i:
                                pe.wait_ge(s["logits_read"], 1)
                            if i:
                                pe.wait_ge(s["xnT_ready"], 1)
                            turn_four(lambda t: x_in[:, 4 * i + t, :], ahead_ps, "xn_turned")
                        elif part in (4, 5, 6):
                            g = part - 4
                            if g == 0:
                                pe.wait_ge(s["xnT_ready"], 2)
                            else:
                                pe.wait_ge(s["proj_ready"], g)
                            for t in range(3 * g, min(3 * g + 3, NT)):
                                ins = nc.tensor.matmul(ahead_ps[:, (t - 3 * g) * NP:(t - 3 * g + 1) * NP],
                                                       next_xT[:, t * P:(t + 1) * P], w_proj[:], start=True, stop=True)
                            ins.then_inc(s["proj_done"], 1)
                        elif part == 9:
                            geometry_twice()
                        elif part == 10:
                            params_twice()

                    def geometry_twice():
                        pe.wait_ge(s["geometry"], 1)
                        pe.wait_ge(s["proj_ready"], 3)
                        for hf in range(2):
                            ins = nc.tensor.matmul(ahead_ps[:, hf * NG:(hf + 1) * NG], pick[:, hf, :], token[:, 0:NG],
                                                   start=True, stop=True)
                        ins.then_inc(s["geometry_twice"], 1)

                    def params_twice():
                        pe.wait_ge(s["params"], 1)
                        pe.wait_ge(s["geometry_out"], 1)
                        for hf in range(2):
                            nc.tensor.matmul(ahead_ps[:, 2 * NG + hf * NR:2 * NG + (hf + 1) * NR], pick[:, hf, :],
                                             token[:, NG:NG + NR], start=True, stop=True)
                        nc.tensor.transpose(ahead_ps[0:NT * NH, MAX_AT:MAX_AT + P],
                                            neg_max[:].rearrange("p t h -> p (t h)"), ident[:]
                                            ).then_inc(s["params_twice"], 1)

                    def exponent(n):
                        j, i = SLOTS[n]
                        k = j % 2
                        if i == 0 and j >= 2:
                            pe.wait_ge(s["window_ready"], j - 1)
                            pe.wait_ge(s["slopes_ready"], j - 1)
                        if i == 0 and j >= 4:
                            pe.wait_ge(max_rows[j // 2 % 2], 32 * (j // 4))
                        if n >= NX:
                            pe.wait_ge(s["weights_ready"], n - NX + 1)
                        cols = slice(i * P, (i + 1) * P)
                        nc.tensor.matmul(turn[n % NX][:], dist[:, k, cols],
                                         slope_diag[:, k].rearrange("p h l -> p (h l)"), start=True, stop=False)
                        nc.tensor.matmul(turn[n % NX][:], miss[:, k, cols],
                                         miss_diag[:, j // 2 % 2, :, k * HB:(k + 1) * HB], start=False, stop=True
                                         ).then_inc(s["exponents"], 1)

                    def product(n):
                        j, i = SLOTS[n]
                        copy, c0, _, chunks = window(j)
                        pe.wait_ge(s["weights_ready"], n + 1)
                        if copy and i == 0:
                            pe.wait_ge(s["rows_moved"], 64)
                        if i == 0 and j % 2 == 0 and j:
                            pe.wait_ge(s["gathered"], j // 2)
                        rows_of = xn[:, c0 + i, :] if copy == 0 else moved[:, copy - 1, c0 + i, :]
                        for g in range(4):
                            ins = nc.tensor.matmul(mixed[32 * g:32 * g + 32, j % 2 * P:(j % 2 + 1) * P],
                                                   rows_of[:, 32 * g:32 * g + 32], weightT[:, n % NWT, g * P:(g + 1) * P],
                                                   start=i == 0, stop=i == chunks - 1)
                        ins.then_inc(s["mixed_slot"], 1)

                    def unit_up(n):
                        m, k = n // NHC, n % NHC
                        hf, e = expert_of(m)
                        cols = slice(hf * HALF, (hf + 1) * HALF)
                        if k == 0 and m % (NE + 1) == 0:
                            pe.wait_ge(s["hi_ready"], 2)
                            pe.wait_ge(s["lo_ready"], 2)
                        if n >= 2:
                            pe.wait_ge(s["silu_done"], n - 1)
                        hs = slice(k * P, (k + 1) * P)
                        nc.tensor.matmul(up[n % 2][:], w1_hi[:, e, hs], xT_hi[:, cols], start=True, stop=False)
                        nc.tensor.matmul(up[n % 2][:], w1_hi[:, e, hs], xT_lo[:, cols], start=False, stop=False)
                        nc.tensor.matmul(up[n % 2][:], w1_lo[:, e, hs], xT_hi[:, cols], start=False, stop=True
                                         ).then_inc(s["up_done"], 1)

                    def unit_down(n):
                        m, t = n // NTU, n % NTU
                        _, e = expert_of(m)
                        if t == 0:
                            pe.wait_ge(s["silu_done"], NHC * (m + 1))
                            if m:
                                pe.wait_ge(s["acc_done"], m)
                        for k in range(NHC):
                            ins = nc.tensor.matmul(down[:, t * C:(t + 1) * C],
                                                   hidden[:, m % 2, k, t * P:(t + 1) * P], w2T[:, e, k, :],
                                                   start=k == 0, stop=k == NHC - 1)
                        if t == NTU - 1:
                            ins.then_inc(s["down_done"], 1)

                    def post(part):
                        if part == 0:
                            pe.wait_ge(s["wide_ready"], 1)
                            pe.wait_ge(s["weights_ready"], NS)
                            turn_all(lambda t: rdenom_wide[:, t * NH:(t + 1) * NH, :].rearrange("p h d -> p (h d)"),
                                     turn[0:2], "rdenom_turned")
                            return
                        for i in range(2):
                            half = slice(i * HALF, (i + 1) * HALF)
                            if part == 1:
                                pe.wait_ge(s["mix_ready"], i + 1)
                                nc.tensor.matmul(gate_ps[i][0:C // 4, :], se1_w[:], xnT[:, half],
                                                 start=True, stop=True).then_inc(s["se1_done"], 1)
                            elif part == 2:
                                pe.wait_ge(s["se1_ready"], i + 1)
                                nc.tensor.matmul(turn[i][:], se2_w[:], se_lin[:, half],
                                                 start=True, stop=True).then_inc(s["se2_done"], 1)
                            elif part == 3 + i:
                                pe.wait_ge(s["gated"], i + 1)
                                for t in range(4):
                                    col = i * HALF + t * P
                                    ins = nc.tensor.matmul(turn[i][:, t * C:(t + 1) * C], xnT[:, col:col + P],
                                                           out_w[:], start=True, stop=True)
                                ins.then_inc(s["out_done"], 1)

                    for what, n in plan:
                        if what == "weights":
                            turn_weights(n)
                        elif what == "ffn head" and n == 0:
                            ffn_turn()
                        elif what == "ffn head" and n == 1:
                            ffn_logits()
                        elif what == "ahead":
                            prepare(n)
                        elif what == "exponent":
                            exponent(n)
                        elif what == "product":
                            product(n)
                        elif what == "up":
                            unit_up(n)
                        elif what == "down part":
                            unit_down(n)
                        elif what == "post":
                            post(n)

                @block.vector
                def _(dve):
                    seq = Chain(dve, s["dve_seq"])
                    V = nc.vector

                    def step_of(ins):
                        seq(ins)
                        seq.wait()

                    def over(a, n):
                        return a.unsqueeze(2).broadcast_to([P, a.shape[1], n])

                    def norm(a, src, var_done):
                        for t in range(NT):
                            ins = V.bn_stats(stats[:, a, t, :], src[:, t, :])
                        step_of(ins)
                        for t in range(NT):
                            ins = V.bn_aggr(mean_var[:, a, t, :], stats[:, a, t, :])
                        step_of(ins)
                        V.tensor_scalar(var_eps[:, a], mean_var[:, a, :, 1], EPS, None, ALU.add
                                        ).then_inc(s[var_done], 1)

                    def normalize(a, src, dst, rstd_done, done):
                        dve.wait_ge(s[rstd_done], 1)
                        for t in range(NT):
                            ins = V.tensor_scalar(dst[:, t, :], src[:, t, :], mean_var[:, a, t, 0:1],
                                                  rstd[:, a, t:t + 1], ALU.subtract, ALU.mult)
                        ins.then_inc(s[done], 1)

                    def choose():
                        dve.wait_ge(s["logits_done"], 1)
                        V.tensor_copy(logits[:].rearrange("p t e -> p (t e)"), ahead_ps[:, 0:NT * NE]
                                      ).then_inc(s["logits_read"], 1)
                        dve.wait_ge(s["logits_read"], 1)
                        for t in range(NT):
                            ins = V.max(out=top[:, t, :], in_=logits[:, t, :])
                        step_of(ins)
                        V.tensor_tensor(gap[:], top[:, :, 1], top[:, :, 0], ALU.subtract
                                        ).then_inc(s["gap_ready"], 1)
                        for t in range(NT):
                            ins = V.max_index(out=top_id[:, t, :], in_max=top[:, t, :], in_values=logits[:, t, :])
                        step_of(ins)
                        V.tensor_copy(top_idf[:], top_id[:])

                    def gate_table():
                        dve.wait_ge(s["gap_tanh"], 1)
                        V.tensor_scalar(gate12[:, 0], gap[:], -0.5, 0.5, ALU.mult, ALU.add)
                        step_of(V.tensor_scalar(gate12[:, 1], gap[:], 0.5, 0.5, ALU.mult, ALU.add))
                        for i, dst in enumerate((gates, picked)):
                            step_of(V.tensor_tensor(dst[:], expert_ids[:].unsqueeze(1).broadcast_to([P, NT, NE]),
                                                    over(top_idf[:, :, i], NE), ALU.is_equal))
                            step_of(V.tensor_tensor(dst[:], dst[:], over(gate12[:, i], NE), ALU.mult))
                        seq(V.tensor_tensor(gates[:], gates[:], picked[:], ALU.add))

                    def ffn_low():
                        for i in range(2):
                            half = slice(i * HALF, (i + 1) * HALF)
                            dve.wait_ge(s["hi_ready"], i + 1)
                            dve.wait_ge(s["xn2T_ready"], i + 1)
                            V.tensor_tensor(xT_lo[:, half], xn2T[:, half], xT_hi[:, half].bitcast(F32),
                                            ALU.subtract).then_inc(s["lo_ready"], 1)

                    def prepare(part):
                        if part == 0:
                            if attention:
                                dve.wait_ge(s["x_loaded"], 16)
                            norm(0, x_in, "var_ready")
                        elif part == 1:
                            normalize(0, x_in, x_in, "rstd_ready", "x_ready")
                        elif part in (4, 5, 6):
                            g = part - 4
                            nt = min(3, NT - 3 * g)
                            dve.wait_ge(s["proj_done"], g + 1)
                            if ffn and g == 0:
                                dve.wait_ge(s["logits_done"], 1)
                                dve.wait_ge(s["lo_ready"], 2)
                            V.tensor_tensor(proj[:, 3 * g:3 * g + nt, :],
                                            ahead_ps[:, 0:nt * NP].rearrange("p (t n) -> p t n", n=NP),
                                            bias_proj[:].unsqueeze(1).broadcast_to([P, nt, NP]), ALU.add
                                            ).then_inc(s["proj_ready"], 1)
                        elif part == 7:
                            silus()
                        elif part == 8:
                            geometry()
                        elif part == 9:
                            parameters()
                        elif part == 10:
                            parameters_twice()
                        elif part in (11, 12):
                            base(part - 11, first=True)

                    def silus():
                        dve.wait_ge(s["tanh_ready"], 1)
                        step_of(V.tensor_scalar(half_tanh, half_tanh, 0.5, 0.5, ALU.mult, ALU.add))
                        V.tensor_tensor(proj, proj, half_tanh, ALU.mult).then_inc(s["silu_ready"], 1)
                        dve.wait_ge(s["silu_ready"], 1)
                        qw = half_tanh[:, :, 0:NQ]
                        step_of(V.tensor_tensor(qw, proj[:, :, NW:NP],
                                                key_w[:].rearrange("p h d -> p (h d)").unsqueeze(1).broadcast_to([P, NT, NQ]),
                                                ALU.mult))
                        seq(V.tensor_reduce(qk[:], qw.rearrange("p t (h d) -> p t h d", d=D), AX, ALU.add))

                    def geometry():
                        dve.wait_ge(s["wave_ready"], 1)
                        step_of(V.tensor_reduce(wave_sum[:], wave[:], AX, ALU.add))
                        V.tensor_scalar(freq, wave_sum[:, :, 0], 7.5 / NH, 8.5, ALU.mult, ALU.add)
                        V.tensor_scalar(phase, wave_sum[:, :, 1], 16.0 / NH, None, ALU.mult)
                        step_of(V.tensor_scalar(decay[:], wave_sum[:, :, 2], 4.75 / NH, 5.25, ALU.mult, ALU.add))
                        V.reciprocal(rfreq, freq)
                        V.tensor_tensor(shift[:], centers, phase, ALU.add)
                        step_of(V.tensor_scalar(decay[:], decay[:], 0.1, None, ALU.max))
                        V.reciprocal(rdecay[:], decay[:])
                        step_of(V.tensor_scalar(shift[:], shift[:], -1.0, 0.5, ALU.mult, ALU.add))
                        V.tensor_tensor(shift2, shift[:], rfreq, ALU.mult).then_inc(s["geometry"], 1)
                        dve.wait_ge(s["geometry"], 1)

                    def parameters():
                        V.tensor_tensor(freq_decay[:], freq, rdecay[:], ALU.mult)
                        V.scalar_tensor_tensor(slope_s[:], qk[:], D ** -0.5, over(freq, NH), ALU.mult, ALU.mult)
                        step_of(V.tensor_tensor(pos[:], over(freq, 2 * MAXK + 1),
                                                strides[:].unsqueeze(1).broadcast_to([P, NT, 2 * MAXK + 1]), ALU.mult))
                        V.tensor_tensor(slope_e, slope_s[:], over(freq_decay[:], NH), ALU.subtract)
                        dve.wait_ge(s["geometry_twice"], 1)
                        V.tensor_copy(twice[:, :, 0:NG], ahead_ps[:, 0:2 * NG].rearrange("p (a n) -> p a n", a=2)
                                      ).then_inc(s["geometry_out"], 1)
                        step_of(V.tensor_tensor(pos[:], pos[:], over(centers, 2 * MAXK + 1), ALU.add))
                        step_of(V.tensor_tensor(pos[:], pos[:], over(phase, 2 * MAXK + 1), ALU.add))
                        step_of(V.tensor_scalar(valid[:], pos[:], 0.0, None, ALU.is_ge))
                        step_of(V.scalar_tensor_tensor(valid[:].rearrange("p t k -> p (t k)"),
                                                       pos[:].rearrange("p t k -> p (t k)"), float(L),
                                                       valid[:].rearrange("p t k -> p (t k)"),
                                                       ALU.is_lt, ALU.mult))
                        V.tensor_copy(some[:, :, 0:1], valid[:, :, 0:1])
                        step_of(V.tensor_tensor(some[:, :, 1:NK], valid[:, :, 1:NK], valid[:, :, NK:], ALU.add))
                        step_of(V.tensor_scalar(valid[:, :, 0:NK], some[:], 0.0, None, ALU.is_gt))
                        V.tensor_tensor(some2[:], valid[:, :, 0:NK],
                                        strides[:, 0:NK].unsqueeze(1).broadcast_to([P, NT, NK]), ALU.mult)
                        step_of(V.tensor_tensor(valid[:, :, 0:NK], valid[:, :, 0:NK],
                                                falling[:].unsqueeze(1).broadcast_to([P, NT, NK]), ALU.mult))
                        V.tensor_reduce(kmax, some2[:], AX, ALU.max)
                        step_of(V.tensor_reduce(kmin, valid[:, :, 0:NK], AX, ALU.max))
                        step_of(V.tensor_scalar(kmin, kmin, -1.0, float(MAXK), ALU.mult, ALU.add))
                        step_of(V.tensor_tensor(kept[:], strides[:, 0:NK].unsqueeze(1).broadcast_to([P, NT, NK]),
                                                over(kmin, NK), ALU.max))
                        V.tensor_tensor(kept[:], kept[:], over(kmax, NK), ALU.min)
                        V.tensor_tensor(end1[:], slope_s[:], over(kmax, NH), ALU.mult)
                        step_of(V.tensor_tensor(end2[:], slope_s[:], over(kmin, NH), ALU.mult))
                        step_of(V.tensor_tensor(end1[:], end1[:], end2[:], ALU.max))
                        V.tensor_scalar(neg_max[:], end1[:], -1.0, None, ALU.mult).then_inc(s["params"], 1)
                        dve.wait_ge(s["params"], 1)

                    def parameters_twice():
                        if attention:
                            for done in max_rows:
                                dve.wait_ge(done, 16 * (NT - 2))
                        dve.wait_ge(s["params_twice"], 1)
                        late = ahead_ps[:, 2 * NG:2 * NG + 2 * NR].rearrange("p (a n) -> p a n", a=2)
                        V.tensor_copy(twice[:, :, NG:], late[:, :, 0:2 * NT])
                        seq(V.tensor_copy(slope_parts[:], late[:, :, 2 * NT:]))
                        step_of(V.tensor_copy(max_parts[:, 0, :], ahead_ps[0:NT * NH, MAX_AT:MAX_AT + P]))
                        V.tensor_tensor(max_parts[:, 1, :], ahead_ps[0:NT * NH, MAX_AT:MAX_AT + P],
                                        max_parts[:, 0, :].bitcast(F32), ALU.subtract).then_inc(s["max_ready"], 1)
                        seq.wait()
                        low = slope_parts[HB:P]
                        V.tensor_tensor(low, late[HB:P, :, 2 * NT:], low.bitcast(F32), ALU.subtract
                                        ).then_inc(s["parts_ready"], 1)

                    def base(j, first=False):
                        _, _, lo, chunks = window(j)
                        w = chunks * P
                        k = j % 2
                        of = twice[:, k].rearrange("p (i t) -> p i t", t=NT)[:, :, j // 2:j // 2 + 1]
                        if first:
                            dve.wait_ge(s["first_candidates"], j + 1)
                            seq.wait()
                        else:
                            dve.wait_ge(s["candidates"], j - 1)
                        wait_exponents(j, first)
                        p, d = place[:, k, 0:w], dist[:, k, 0:w]
                        r = samp[:, k, 0:w]
                        step_of(V.tensor_scalar(r, r, MAGIC + MAXK, MAGIC, ALU.min, ALU.subtract))
                        step_of(V.tensor_scalar(p, r[0:HB], of[0:HB, 0], of[0:HB, 2], ALU.mult, ALU.add))
                        bits = r.bitcast(U32)
                        seq(V.tensor_scalar(bits, bits, 0x7FFFFFFF, None, ALU.bitwise_and))
                        step_of(V.scalar_tensor_tensor(p, p, of[0:HB, 1], rows[0:HB, lo:lo + w],
                                                       ALU.add, ALU.subtract))
                        V.tensor_scalar(d, r, of[:, 5], of[:, 6], ALU.min, ALU.max)
                        step_of(V.tensor_scalar(above[:, 0:w], p, 1.0, None, ALU.is_ge))
                        V.scalar_tensor_tensor(miss[0:HB, k, 0:w], p, 0.0, above[:, 0:w], ALU.is_lt, ALU.add
                                               ).then_inc(s["first_windows" if first else "window_ready"], 1)

                    def wait_exponents(j, first):
                        if not first:
                            dve.wait_ge(s["exponents"], SLOTS_BEFORE[j - 1])
                        elif attention:
                            dve.wait_ge(s["exponents"], SLOTS_BEFORE[NJ - 1 + j])

                    def denominators():
                        dve.wait_ge(s["sums_masked"], 2)
                        step_of(V.tensor_reduce(sum_zu[:], sums[:], AX, ALU.add))
                        step_of(V.scalar_tensor_tensor(denom[:], sum_zu[:, 0], 1e-8, sum_zu[:, 1], ALU.mult, ALU.add))
                        step_of(V.reciprocal(rdenom[:], denom[:]))
                        V.tensor_copy(rdenom_wide, over(rdenom[:], D)).then_inc(s["wide_ready"], 1)

                    def gather(t):
                        dve.wait_ge(s["mixed_slot"], SLOTS_BEFORE[2 * t + 2])
                        part = mixed[:, 0:2 * P].rearrange("p (j q l) -> p q j l", j=2, q=2)
                        dst = xnT[:, t * P:(t + 1) * P].rearrange("p (j l) -> p j l", j=2)
                        step_of(V.tensor_scalar(dst, part[:, 0], parity[:, 0:1], None, ALU.mult))
                        V.scalar_tensor_tensor(dst, part[:, 1], parity[:, 1:2], dst, ALU.mult, ALU.add
                                               ).then_inc(s["gathered"], 1)

                    def unit(m):
                        hf, e = expert_of(m)
                        dve.wait_ge(s["down_done"], m + 1)
                        if m == 1:
                            seq.wait()
                        if m % (NE + 1):
                            dve.wait_ge(s["acc_done"], m)
                        t0 = hf * NT // 2
                        if e == NE:
                            V.tensor_tensor(acc[:, t0:t0 + NT // 2, :].rearrange("p t c -> p (t c)"), down[:],
                                            x1[:, t0:t0 + NT // 2, :].rearrange("p t c -> p (t c)"), ALU.add
                                            ).then_inc(s["acc_done"], 1)
                            return
                        for t in range(NT // 2):
                            a = acc[:, t0 + t, :]
                            ins = V.scalar_tensor_tensor(a, down[:, t * C:(t + 1) * C],
                                                         gates[:, t0 + t, e:e + 1], a, ALU.mult, ALU.add)
                        ins.then_inc(s["acc_done"], 1)

                    def post(part):
                        if part == 0:
                            dve.wait_ge(s["gathered"], NT)
                            for i in range(2):
                                half = slice(i * HALF, (i + 1) * HALF)
                                dve.wait_ge(s["rdenom_turned"], i + 1)
                                V.tensor_tensor(xnT[:, half], xnT[:, half], turn[i][:], ALU.mult
                                                ).then_inc(s["mix_ready"], 1)
                            return
                        for i in range(2):
                            half = slice(i * HALF, (i + 1) * HALF)
                            if part == 1:
                                dve.wait_ge(s["se1_tanh"], i + 1)
                                step_of(V.tensor_scalar(se_lin[:, half], gate_ps[i][0:C // 4, :],
                                                        se1_b[:, 0:1], 0.5, ALU.add, ALU.mult))
                                V.scalar_tensor_tensor(se_lin[:, half], se_tanh[:, half], 1.0, se_lin[:, half],
                                                       ALU.add, ALU.mult).then_inc(s["se1_ready"], 1)
                            elif part == 2:
                                dve.wait_ge(s["se2_tanh"], i + 1)
                                V.scalar_tensor_tensor(xnT[:, half], se_gate[:, half], 1.0, xnT[:, half],
                                                       ALU.add, ALU.mult).then_inc(s["gated"], 1)
                            elif part == 3 + i:
                                if i == 0:
                                    dve.wait_ge(s["res_loaded"], 16)
                                dve.wait_ge(s["out_tanh_ready"], i + 1)
                                step_of(V.scalar_tensor_tensor(attn[:, half], out_tanh[:, half], 1.0, turn[i][:],
                                                               ALU.add, ALU.mult))
                                V.scalar_tensor_tensor(x1[:, 4 * i:4 * i + 4, :].rearrange("p t c -> p (t c)"),
                                                       attn[:, half], 0.5,
                                                       x_res[:, 4 * i:4 * i + 4, :].rearrange("p t c -> p (t c)"),
                                                       ALU.mult, ALU.add)

                    for what, n in plan:
                        if what == "weights" and n <= NE:
                            dve.wait_ge(s["weights_hi"], n + 1)
                            V.tensor_tensor(w1_lo[:, n, :], up[n % 2][:], w1_hi[:, n, :].bitcast(F32),
                                            ALU.subtract).then_inc(s["weights_free"], 1)
                        elif what == "ffn norm" and n == 0:
                            norm(1, x1, "var2_ready")
                        elif what == "ffn norm":
                            normalize(1, x1, xn2, "rstd2_ready", "xn2_ready")
                        elif what == "ffn head" and n == 0:
                            ffn_low()
                        elif what == "ffn head" and n == 1:
                            choose()
                        elif what == "ffn head" and n == 3:
                            gate_table()
                        elif what == "ahead":
                            prepare(n)
                        elif what == "window":
                            base(n)
                        elif what == "sums" and n == 7:
                            denominators()
                        elif what == "gather":
                            gather(n)
                        elif what == "down":
                            unit(n)
                        elif what == "post":
                            post(n)
            clear_semaphores()

        setup()
        clear_semaphores()
        step(-1, False, False, True)
        step(0, True, False, True)
        with nc.Fori(1, B) as b:
            step(b, True, True, True)
        step(B, False, True, False)


_INS = ['L0_attn_x', 'L0_attn_w_wave', 'L0_attn_b_wave', 'L0_attn_w_query', 'L0_attn_b_query',
        'L0_attn_key_weight', 'L0_attn_w_se1', 'L0_attn_b_se1', 'L0_attn_w_se2', 'L0_attn_b_se2',
        'L0_attn_w_out', 'L0_ffn_shared_w1', 'L0_ffn_shared_w2', 'L0_ffn_experts_w1',
        'L0_ffn_experts_w2', 'L0_ffn_gate_w']


def kernel(**inputs):
    import numpy as np
    import concourse.bacc as bacc
    from concourse.bass_utils import run_bass_kernel_spmd

    nc = bacc.Bacc("TRN2", target_bir_lowering=False, num_devices=1)
    arrays, args = {}, []
    for name in _INS:
        a = np.ascontiguousarray(inputs[name])
        arrays[f"in_{name}"] = a
        args.append(nc.dram_tensor(f"in_{name}", a.shape, mybir.dt.from_np(a.dtype), kind="ExternalInput").ap())
    shape = inputs['L0_attn_x'].shape
    result = nc.dram_tensor("out_x", shape, mybir.dt.float32, kind="ExternalOutput").ap()
    build_program(nc, *args, result)
    r = run_bass_kernel_spmd(nc, [arrays], core_ids=[0])
    return r.results[0]["out_x"]
```
